# Optimizing a Trainium2 kernel written in Bass

```python
import numpy as np
import jax
import jax.numpy as jnp

def _softmax(x, axis=-1):
    return jax.nn.softmax(x, axis=axis)

def _gelu(x):
    return jax.nn.gelu(x, approximate=True)

def _silu(x):
    return jax.nn.silu(x)

def _sigmoid(x):
    return jax.nn.sigmoid(x)

def _layernorm(x, axis=-1, eps=1e-05):
    m = jnp.mean(x, axis=axis, keepdims=True)
    v = jnp.var(x, axis=axis, keepdims=True)
    return (x - m) / jnp.sqrt(v + eps)

def _scatter_add(tgt, idx, src, axis=0):
    return tgt.at[idx].add(src)

def _segment_sum(src, seg, n):
    return jax.ops.segment_sum(src, seg, n)
kernel_name = 'mk_seq_postln_d2_jaxref_r8_0dafae'

def setup_inputs(seed: int=0):
    np.random.seed(seed)
    _w = jnp.asarray

    def _L0_attn_setup():
        import jax, jax.numpy as jnp
        import numpy as np
        B, S, D = (1, 256, 512)
        H = 32
        QL = 192
        KVL = 64
        DN = 128
        DR = 64
        DV = 128
        BASE = 10000.0
        FACTOR = 40.0
        BFAST, BSLOW = (32.0, 1.0)
        OLD_CTX = 4096.0
        MSCALE = 1.0

        def _yarn_inv_freq():
            freqs = 1.0 / BASE ** (jnp.arange(0, DR, 2, dtype=jnp.float32) / DR)
            wavelengths = 2.0 * jnp.pi / freqs
            ramp = jnp.clip((wavelengths / OLD_CTX - BSLOW) / (BFAST - BSLOW), 0.0, 1.0)
            scale = 1.0 - ramp + ramp * FACTOR
            return (freqs / scale, MSCALE)

        def _apply_rope(x, inv_freq, mscale):
            seq = x.shape[-2]
            pos = jnp.arange(seq, dtype=jnp.float32)
            f = jnp.concatenate([pos[:, None] * inv_freq[None, :]] * 2, axis=-1)
            cos = jnp.cos(f) * mscale
            sin = jnp.sin(f) * mscale
            half = DR // 2
            x1, x2 = (x[..., :half], x[..., half:])
            c1, c2 = (cos[:, :half], cos[:, half:])
            s2 = sin[:, half:]
            return jnp.concatenate([x1 * c1 - x2 * s2, x1 * s2 + x2 * c2], axis=-1)
        key = jax.random.key(seed)
        ks = jax.random.split(key, 10)

        def glorot(k, shape):
            lim = np.sqrt(6.0 / (shape[0] + shape[1])).astype(np.float32)
            return jax.random.uniform(k, shape, jnp.float32, -lim, lim)
        return {'hidden_states': jax.random.normal(ks[0], (B, S, D), jnp.float32), 'w_q_down': glorot(ks[1], (D, QL)), 'w_q_up_nope': glorot(ks[2], (QL, H * DN)), 'w_q_up_rope': glorot(ks[3], (QL, H * DR)), 'w_kv_down': glorot(ks[4], (D, KVL)), 'w_k_rope': glorot(ks[5], (D, DR)), 'w_uk': glorot(ks[6], (H * DN, KVL)), 'w_uv': glorot(ks[7], (H * DV, KVL)), 'w_out': glorot(ks[8], (H * DV, D))}
    _L0_attn_in = _L0_attn_setup()

    def _L0_ffn_setup():
        import jax, jax.numpy as jnp
        import numpy as np
        HIDDEN = 512
        INTER = 1376
        GROUP = 128
        B, S = (4, 256)
        NIB = jnp.uint32(15)

        def _pack_rows(nib):
            r = nib.reshape(-1, 8, nib.shape[-1])
            shifts = (jnp.arange(8, dtype=jnp.uint32) * 4)[None, :, None]
            return jnp.sum(r << shifts, axis=1, dtype=jnp.uint32)

        def _pack_cols(nib):
            r = nib.reshape(nib.shape[0], -1, 8)
            shifts = (jnp.arange(8, dtype=jnp.uint32) * 4)[None, None, :]
            return jnp.sum(r << shifts, axis=2, dtype=jnp.uint32)

        def _dequant(qw, qz, sc, g_idx):
            shifts = jnp.arange(8, dtype=jnp.uint32) * 4
            wq = qw[:, None, :] >> shifts[None, :, None] & NIB
            wq = wq.reshape(-1, qw.shape[1]).astype(jnp.float32)
            zq = qz[:, :, None] >> shifts[None, None, :] & NIB
            zq = zq.reshape(qz.shape[0], -1).astype(jnp.float32) + 1.0
            return sc[g_idx] * (wq - zq[g_idx])
        key = jax.random.key(seed)
        ks = jax.random.split(key, 7)
        n_groups = HIDDEN // GROUP
        n_groups_d = INTER // GROUP
        x = jax.random.normal(ks[0], (B, S, HIDDEN), jnp.float32)
        nib_w_gu = jax.random.randint(ks[1], (HIDDEN, 2 * INTER), 0, 16).astype(jnp.uint32)
        nib_z_gu = jax.random.randint(ks[2], (n_groups, 2 * INTER), 0, 15).astype(jnp.uint32)
        qweight_gu = _pack_rows(nib_w_gu)
        qzeros_gu = _pack_cols(nib_z_gu)
        scales_gu = jax.random.uniform(ks[3], (n_groups, 2 * INTER), jnp.float32, 0.005, 0.02)
        g_idx_gu = jnp.arange(HIDDEN, dtype=jnp.int32) // GROUP
        nib_w_d = jax.random.randint(ks[4], (INTER, HIDDEN), 0, 16).astype(jnp.uint32)
        nib_z_d = jax.random.randint(ks[5], (n_groups_d, HIDDEN), 0, 15).astype(jnp.uint32)
        qweight_down = _pack_rows(nib_w_d)
        qzeros_down = _pack_cols(nib_z_d)
        scales_down = jax.random.uniform(ks[6], (n_groups_d, HIDDEN), jnp.float32, 0.005, 0.02)
        g_idx_down = jnp.arange(INTER, dtype=jnp.int32) // GROUP
        return {'x': x, 'qweight_gu': qweight_gu, 'qzeros_gu': qzeros_gu, 'scales_gu': scales_gu, 'g_idx_gu': g_idx_gu, 'qweight_down': qweight_down, 'qzeros_down': qzeros_down, 'scales_down': scales_down, 'g_idx_down': g_idx_down}
    _L0_ffn_in = _L0_ffn_setup()

    def _L1_attn_setup():
        import jax, jax.numpy as jnp
        import numpy as np
        B, S, D = (2, 128, 512)
        H, KVH, HD = (32, 8, 128)
        GROUPS = H // KVH
        LAT, LH = (128, 32)
        THETA = 10000.0
        SCALE = 1.0 / float(np.sqrt(HD))

        def _rope_cos_sin(seq_len, head_dim, theta):
            inv_freq = 1.0 / theta ** (jnp.arange(0, head_dim, 2, dtype=jnp.float32) / head_dim)
            t = jnp.arange(seq_len, dtype=jnp.float32)
            freqs = jnp.outer(t, inv_freq)
            emb = jnp.concatenate([freqs, freqs], axis=-1)
            return (jnp.cos(emb), jnp.sin(emb))

        def _rotate_half(x):
            h = x.shape[-1] // 2
            return jnp.concatenate([-x[..., h:], x[..., :h]], axis=-1)

        def _apply_rope(x, cos, sin):
            return x * cos[None, None] + _rotate_half(x) * sin[None, None]

        def _causal_attn(q, k, v, scale):
            s = jnp.einsum('bhqd,bhkd->bhqk', q, k) * scale
            mask = jnp.tril(jnp.ones((q.shape[2], k.shape[2]), dtype=bool))
            s = jnp.where(mask[None, None], s, jnp.finfo(s.dtype).min)
            p = jax.nn.softmax(s, axis=-1)
            return jnp.einsum('bhqk,bhkd->bhqd', p, v)
        key = jax.random.key(seed)
        ks = jax.random.split(key, 9)
        sd = 0.02
        mk = lambda k, shape: jax.random.normal(k, shape, dtype=jnp.float32) * sd
        return {'hidden_states': jax.random.normal(ks[0], (B, S, D), dtype=jnp.float32), 'w_q': mk(ks[1], (D, H * HD)), 'w_k': mk(ks[2], (D, KVH * HD)), 'w_v': mk(ks[3], (D, KVH * HD)), 'w_o': mk(ks[4], (H * HD, D)), 'w_lq': mk(ks[5], (D, LAT)), 'w_lk': mk(ks[6], (LAT, LH * HD)), 'w_lv': mk(ks[7], (D, LH * HD)), 'w_lo': mk(ks[8], (LH * HD, D))}
    _L1_attn_in = _L1_attn_setup()

    def _L1_ffn_setup():
        import jax, jax.numpy as jnp
        import numpy as np
        NF4_CODE = jnp.array([-1.0, -0.6961928009986877, -0.5250730514526367, -0.39491748809814453, -0.28444138169288635, -0.18477343022823334, -0.09105003625154495, 0.0, 0.07958029955625534, 0.16093020141124725, 0.24611230194568634, 0.33791524171829224, 0.44070982933044434, 0.5626170039176941, 0.7229568362236023, 1.0], dtype=jnp.float32)
        BLOCKSIZE = 64

        def nf4_quant_dequant(w):
            shape = w.shape
            flat = w.reshape(-1, BLOCKSIZE)
            absmax = jnp.max(jnp.abs(flat), axis=1, keepdims=True)
            normalized = flat / jnp.where(absmax == 0, 1.0, absmax)
            bounds = (NF4_CODE[:-1] + NF4_CODE[1:]) * 0.5
            idx = jnp.searchsorted(bounds, normalized)
            return (NF4_CODE[idx] * absmax).reshape(shape)
        key = jax.random.key(seed)
        k1, k2, k3, kx = jax.random.split(key, 4)
        D, H = (512, 1376)
        scale = 0.02
        w1 = jax.random.normal(k1, (H, D), jnp.float32) * scale
        w2 = jax.random.normal(k2, (H, D), jnp.float32) * scale
        w3 = jax.random.normal(k3, (D, H), jnp.float32) * scale
        x = jax.random.normal(kx, (2, 256, D), jnp.float32)
        return {'x': x, 'w1': w1, 'w2': w2, 'w3': w3}
    _L1_ffn_in = _L1_ffn_setup()
    _d = {'L0_attn_hidden_states': _L0_attn_in['hidden_states'], 'L0_attn_w_q_down': _L0_attn_in['w_q_down'], 'L0_attn_w_q_up_nope': _L0_attn_in['w_q_up_nope'], 'L0_attn_w_q_up_rope': _L0_attn_in['w_q_up_rope'], 'L0_attn_w_kv_down': _L0_attn_in['w_kv_down'], 'L0_attn_w_k_rope': _L0_attn_in['w_k_rope'], 'L0_attn_w_uk': _L0_attn_in['w_uk'], 'L0_attn_w_uv': _L0_attn_in['w_uv'], 'L0_attn_w_out': _L0_attn_in['w_out'], 'L0_ffn_qweight_gu': _L0_ffn_in['qweight_gu'], 'L0_ffn_qzeros_gu': _L0_ffn_in['qzeros_gu'], 'L0_ffn_scales_gu': _L0_ffn_in['scales_gu'], 'L0_ffn_g_idx_gu': _L0_ffn_in['g_idx_gu'], 'L0_ffn_qweight_down': _L0_ffn_in['qweight_down'], 'L0_ffn_qzeros_down': _L0_ffn_in['qzeros_down'], 'L0_ffn_scales_down': _L0_ffn_in['scales_down'], 'L0_ffn_g_idx_down': _L0_ffn_in['g_idx_down'], 'L1_attn_w_q': _L1_attn_in['w_q'], 'L1_attn_w_k': _L1_attn_in['w_k'], 'L1_attn_w_v': _L1_attn_in['w_v'], 'L1_attn_w_o': _L1_attn_in['w_o'], 'L1_attn_w_lq': _L1_attn_in['w_lq'], 'L1_attn_w_lk': _L1_attn_in['w_lk'], 'L1_attn_w_lv': _L1_attn_in['w_lv'], 'L1_attn_w_lo': _L1_attn_in['w_lo'], 'L1_ffn_w1': _L1_ffn_in['w1'], 'L1_ffn_w2': _L1_ffn_in['w2'], 'L1_ffn_w3': _L1_ffn_in['w3']}
    _x0 = _d['L0_attn_hidden_states']
    _d['L0_attn_hidden_states'] = jax.random.normal(jax.random.fold_in(jax.random.key(seed), 1), (4, 256, 512), dtype=_x0.dtype)
    del _x0
    return _d

def reference(L0_attn_hidden_states, L0_attn_w_q_down, L0_attn_w_q_up_nope, L0_attn_w_q_up_rope, L0_attn_w_kv_down, L0_attn_w_k_rope, L0_attn_w_uk, L0_attn_w_uv, L0_attn_w_out, L0_ffn_qweight_gu, L0_ffn_qzeros_gu, L0_ffn_scales_gu, L0_ffn_g_idx_gu, L0_ffn_qweight_down, L0_ffn_qzeros_down, L0_ffn_scales_down, L0_ffn_g_idx_down, L1_attn_w_q, L1_attn_w_k, L1_attn_w_v, L1_attn_w_o, L1_attn_w_lq, L1_attn_w_lk, L1_attn_w_lv, L1_attn_w_lo, L1_ffn_w1, L1_ffn_w2, L1_ffn_w3):

    def _L0_attn_ref(hidden_states, w_q_down, w_q_up_nope, w_q_up_rope, w_kv_down, w_k_rope, w_uk, w_uv, w_out):
        import jax, jax.numpy as jnp
        import numpy as np
        B, S, D = (1, 256, 512)
        H = 32
        QL = 192
        KVL = 64
        DN = 128
        DR = 64
        DV = 128
        BASE = 10000.0
        FACTOR = 40.0
        BFAST, BSLOW = (32.0, 1.0)
        OLD_CTX = 4096.0
        MSCALE = 1.0

        def _yarn_inv_freq():
            freqs = 1.0 / BASE ** (jnp.arange(0, DR, 2, dtype=jnp.float32) / DR)
            wavelengths = 2.0 * jnp.pi / freqs
            ramp = jnp.clip((wavelengths / OLD_CTX - BSLOW) / (BFAST - BSLOW), 0.0, 1.0)
            scale = 1.0 - ramp + ramp * FACTOR
            return (freqs / scale, MSCALE)

        def _apply_rope(x, inv_freq, mscale):
            seq = x.shape[-2]
            pos = jnp.arange(seq, dtype=jnp.float32)
            f = jnp.concatenate([pos[:, None] * inv_freq[None, :]] * 2, axis=-1)
            cos = jnp.cos(f) * mscale
            sin = jnp.sin(f) * mscale
            half = DR // 2
            x1, x2 = (x[..., :half], x[..., half:])
            c1, c2 = (cos[:, :half], cos[:, half:])
            s2 = sin[:, half:]
            return jnp.concatenate([x1 * c1 - x2 * s2, x1 * s2 + x2 * c2], axis=-1)
        b, s, _ = hidden_states.shape
        c_q = hidden_states @ w_q_down
        q_nope = (c_q @ w_q_up_nope).reshape(b, s, H, DN).transpose(0, 2, 1, 3)
        q_rope = (c_q @ w_q_up_rope).reshape(b, s, H, DR).transpose(0, 2, 1, 3)
        c_kv = hidden_states @ w_kv_down
        k_rope = (hidden_states @ w_k_rope)[:, None]
        inv_freq, mscale = _yarn_inv_freq()
        q_rope = _apply_rope(q_rope, inv_freq, mscale)
        k_rope = _apply_rope(k_rope, inv_freq, mscale)
        wuk = w_uk.reshape(H, DN, KVL)
        q_lat = jnp.einsum('bhsd,hdr->bhsr', q_nope, wuk)
        scores = jnp.einsum('bhsr,btr->bhst', q_lat, c_kv) + jnp.einsum('bhsd,btd->bhst', q_rope, k_rope[:, 0])
        scores = scores / jnp.sqrt(jnp.float32(DN + DR))
        causal = jnp.tril(jnp.ones((s, s), dtype=bool))
        scores = jnp.where(causal, scores, jnp.finfo(scores.dtype).min)
        probs = jax.nn.softmax(scores, axis=-1)
        out_lat = jnp.einsum('bhst,btr->bhsr', probs, c_kv)
        wuv = w_uv.reshape(H, DV, KVL)
        out = jnp.einsum('bhsr,hdr->bhsd', out_lat, wuv)
        out = out.transpose(0, 2, 1, 3).reshape(b, s, H * DV)
        return out @ w_out

    def _L0_ffn_ref(x, qweight_gu, qzeros_gu, scales_gu, g_idx_gu, qweight_down, qzeros_down, scales_down, g_idx_down):
        import jax, jax.numpy as jnp
        import numpy as np
        HIDDEN = 512
        INTER = 1376
        GROUP = 128
        B, S = (4, 256)
        NIB = jnp.uint32(15)

        def _pack_rows(nib):
            r = nib.reshape(-1, 8, nib.shape[-1])
            shifts = (jnp.arange(8, dtype=jnp.uint32) * 4)[None, :, None]
            return jnp.sum(r << shifts, axis=1, dtype=jnp.uint32)

        def _pack_cols(nib):
            r = nib.reshape(nib.shape[0], -1, 8)
            shifts = (jnp.arange(8, dtype=jnp.uint32) * 4)[None, None, :]
            return jnp.sum(r << shifts, axis=2, dtype=jnp.uint32)

        def _dequant(qw, qz, sc, g_idx):
            shifts = jnp.arange(8, dtype=jnp.uint32) * 4
            wq = qw[:, None, :] >> shifts[None, :, None] & NIB
            wq = wq.reshape(-1, qw.shape[1]).astype(jnp.float32)
            zq = qz[:, :, None] >> shifts[None, None, :] & NIB
            zq = zq.reshape(qz.shape[0], -1).astype(jnp.float32) + 1.0
            return sc[g_idx] * (wq - zq[g_idx])
        w_gu = _dequant(qweight_gu, qzeros_gu, scales_gu, g_idx_gu)
        inter = jnp.einsum('bsh,hf->bsf', x, w_gu)
        gate, up = (inter[..., :INTER], inter[..., INTER:])
        h = jax.nn.silu(gate) * up
        w_d = _dequant(qweight_down, qzeros_down, scales_down, g_idx_down)
        return jnp.einsum('bsf,fh->bsh', h, w_d)

    def _L1_attn_ref(hidden_states, w_q, w_k, w_v, w_o, w_lq, w_lk, w_lv, w_lo):
        import jax, jax.numpy as jnp
        import numpy as np
        B, S, D = (2, 128, 512)
        H, KVH, HD = (32, 8, 128)
        GROUPS = H // KVH
        LAT, LH = (128, 32)
        THETA = 10000.0
        SCALE = 1.0 / float(np.sqrt(HD))

        def _rope_cos_sin(seq_len, head_dim, theta):
            inv_freq = 1.0 / theta ** (jnp.arange(0, head_dim, 2, dtype=jnp.float32) / head_dim)
            t = jnp.arange(seq_len, dtype=jnp.float32)
            freqs = jnp.outer(t, inv_freq)
            emb = jnp.concatenate([freqs, freqs], axis=-1)
            return (jnp.cos(emb), jnp.sin(emb))

        def _rotate_half(x):
            h = x.shape[-1] // 2
            return jnp.concatenate([-x[..., h:], x[..., :h]], axis=-1)

        def _apply_rope(x, cos, sin):
            return x * cos[None, None] + _rotate_half(x) * sin[None, None]

        def _causal_attn(q, k, v, scale):
            s = jnp.einsum('bhqd,bhkd->bhqk', q, k) * scale
            mask = jnp.tril(jnp.ones((q.shape[2], k.shape[2]), dtype=bool))
            s = jnp.where(mask[None, None], s, jnp.finfo(s.dtype).min)
            p = jax.nn.softmax(s, axis=-1)
            return jnp.einsum('bhqk,bhkd->bhqd', p, v)
        x = hidden_states
        bsz, q_len, _ = x.shape
        q = (x @ w_q).reshape(bsz, q_len, H, HD).transpose(0, 2, 1, 3)
        k = (x @ w_k).reshape(bsz, q_len, KVH, HD).transpose(0, 2, 1, 3)
        v = (x @ w_v).reshape(bsz, q_len, KVH, HD).transpose(0, 2, 1, 3)
        lq = x @ w_lq
        lk = (lq @ w_lk).reshape(bsz, q_len, LH, HD).transpose(0, 2, 1, 3)
        lv = (x @ w_lv).reshape(bsz, q_len, LH, HD).transpose(0, 2, 1, 3)
        cos, sin = _rope_cos_sin(q_len, HD, THETA)
        q = _apply_rope(q, cos, sin)
        k = _apply_rope(k, cos, sin)
        lk = _apply_rope(lk, cos, sin)
        k = jnp.repeat(k, GROUPS, axis=1)
        v = jnp.repeat(v, GROUPS, axis=1)
        attn = _causal_attn(q, k, v, SCALE)
        lat = _causal_attn(q, lk, lv, SCALE)
        attn = attn.transpose(0, 2, 1, 3).reshape(bsz, q_len, H * HD)
        lat = lat.transpose(0, 2, 1, 3).reshape(bsz, q_len, LH * HD)
        return attn @ w_o + lat @ w_lo

    def _L1_ffn_ref(x, w1, w2, w3):
        import jax, jax.numpy as jnp
        import numpy as np
        NF4_CODE = jnp.array([-1.0, -0.6961928009986877, -0.5250730514526367, -0.39491748809814453, -0.28444138169288635, -0.18477343022823334, -0.09105003625154495, 0.0, 0.07958029955625534, 0.16093020141124725, 0.24611230194568634, 0.33791524171829224, 0.44070982933044434, 0.5626170039176941, 0.7229568362236023, 1.0], dtype=jnp.float32)
        BLOCKSIZE = 64

        def nf4_quant_dequant(w):
            shape = w.shape
            flat = w.reshape(-1, BLOCKSIZE)
            absmax = jnp.max(jnp.abs(flat), axis=1, keepdims=True)
            normalized = flat / jnp.where(absmax == 0, 1.0, absmax)
            bounds = (NF4_CODE[:-1] + NF4_CODE[1:]) * 0.5
            idx = jnp.searchsorted(bounds, normalized)
            return (NF4_CODE[idx] * absmax).reshape(shape)
        dq1 = nf4_quant_dequant(w1)
        dq2 = nf4_quant_dequant(w2)
        dq3 = nf4_quant_dequant(w3)
        gate = jnp.einsum('bsd,hd->bsh', x, dq1)
        up = jnp.einsum('bsd,hd->bsh', x, dq2)
        h = jax.nn.silu(gate) * up
        return jnp.einsum('bsh,dh->bsd', h, dq3)
    x = L0_attn_hidden_states
    x = _layernorm(x + _L0_attn_ref(x, L0_attn_w_q_down, L0_attn_w_q_up_nope, L0_attn_w_q_up_rope, L0_attn_w_kv_down, L0_attn_w_k_rope, L0_attn_w_uk, L0_attn_w_uv, L0_attn_w_out), axis=-1)
    x = _layernorm(x + _L0_ffn_ref(x, L0_ffn_qweight_gu, L0_ffn_qzeros_gu, L0_ffn_scales_gu, L0_ffn_g_idx_gu, L0_ffn_qweight_down, L0_ffn_qzeros_down, L0_ffn_scales_down, L0_ffn_g_idx_down), axis=-1)
    x = _layernorm(x + _L1_attn_ref(x, L1_attn_w_q, L1_attn_w_k, L1_attn_w_v, L1_attn_w_o, L1_attn_w_lq, L1_attn_w_lk, L1_attn_w_lv, L1_attn_w_lo), axis=-1)
    x = _layernorm(x + _L1_ffn_ref(x, L1_ffn_w1, L1_ffn_w2, L1_ffn_w3), axis=-1)
    return x

_drawn_inputs = setup_inputs


def setup_inputs(seed=0):
    import zlib

    import numpy as np

    out = dict(_drawn_inputs(seed))
    spreads = {}
    factors = {'L0_attn_w_q_up_nope': 8.0,
     'L0_attn_w_uk': 8.0,
     'L1_attn_w_q': 2.79,
     'L1_attn_w_k': 2.864,
     'L1_attn_w_lq': 8.0,
     'L1_attn_w_lk': 8.0}
    for name, (base, spread) in spreads.items():
        noise = np.random.default_rng([zlib.crc32(name.encode()), seed]).standard_normal(out[name].shape)
        drawn = base * np.exp(spread * noise) if base else spread * noise
        out[name] = jnp.asarray(drawn.astype(out[name].dtype))
    for name, factor in factors.items():
        out[name] = (out[name] * factor).astype(out[name].dtype)
    return out
```

```python
from contextlib import ExitStack

import numpy as np

import concourse.bass as bass
from concourse import mybir

F32 = mybir.dt.float32
R32 = mybir.dt.float32r
U32 = mybir.dt.uint32
I32 = mybir.dt.int32
ALU = mybir.AluOpType
ACT = mybir.ActivationFunctionType
AX_XY = mybir.AxisListType.XY

P = 128
BATCH, SEQ, D = 4, 256, 512
TOK = BATCH * SEQ
TT = TOK // P
KT = D // P
HALF = 512
GROUPS, PER = 8, 4
HEADS = GROUPS * PER
QL, LAT, ROPE = 192, 64, 64
HD = 128
INTER = 1376
FT = 12
EPS = 1e-5
NEG = -3.0e38
STEPS = PER * BATCH


def wait(eng, sem, value):
    if isinstance(value, int) and value <= 0:
        return
    eng.wait_ge(sem, value)


def hold(eng, passed, *waits):
    for sem, value in waits:
        wait(eng, sem, value)
    if any(not isinstance(value, int) for _, value in waits):
        eng.sem_inc(passed, 1)


def product(pe, out, left, right, first, last):
    (lh, ll), (rh, rl) = left, right
    pe.matmul(out, lh, rh, start=first, stop=False)
    pe.matmul(out, lh, rl, start=False, stop=False)
    return pe.matmul(out, ll, rh, start=False, stop=last)


class Pair:

    def __init__(self, ctx, nc, name, shape):
        self.hi = ctx.enter_context(nc.sbuf_tensor(name + "_hi", shape, R32))
        self.lo = ctx.enter_context(nc.sbuf_tensor(name + "_lo", shape, R32))

    def __getitem__(self, key):
        return self.hi[key], self.lo[key]


def transposed_block(nc, tag, X, XT, ident, banks, normalise):
    with ExitStack() as ctx:
        sb = lambda n, s, d: ctx.enter_context(nc.sbuf_tensor(tag + n, s, d))
        sem = lambda n: ctx.enter_context(nc.semaphore(tag + n))
        stats = sb("stats", [P, TT, 6], F32)
        moments = sb("moments", [P, TT, 2], F32)
        root = sb("root", [P, TT], F32)
        inverse = sb("inverse", [P, TT], F32)
        stats_done, moments_done, var_ready = sem("stats_done"), sem("moments_done"), sem("var_ready")
        root_ready, inverse_done = sem("root_ready"), sem("inverse_done")
        x_ready, turned, hi_done, lo_done = sem("x_ready"), sem("turned"), sem("hi_done"), sem("lo_done")
        block = ctx.enter_context(nc.Block())

        def bank_view(t):
            return banks[t % 2][:, :].rearrange("p (k c) -> p k c", k=KT)

        @block.vector
        def _(dve):
            if normalise:
                for t in range(TT):
                    dve.bn_stats(stats[:, t, :], X[:, t, :]).then_inc(stats_done, 1)
                for t in range(TT):
                    dve.wait_ge(stats_done, t + 1)
                    dve.bn_aggr(moments[:, t, :], stats[:, t, :]).then_inc(moments_done, 1)
                dve.wait_ge(moments_done, TT)
                dve.tensor_scalar(root[:, :], moments[:, :, 1], EPS, None, ALU.add).then_inc(var_ready, 1)
                dve.wait_ge(root_ready, 1)
                dve.reciprocal(inverse[:, :], moments[:, :, 1]).then_inc(inverse_done, 1)
                dve.wait_ge(inverse_done, 1)
                for t in range(TT):
                    dve.tensor_scalar(X[:, t, :], X[:, t, :], moments[:, t, 0:1], inverse[:, t:t + 1],
                                      ALU.subtract, ALU.mult).then_inc(x_ready, 1)
            if XT is not None:
                for t in range(TT):
                    dve.wait_ge(hi_done, t + 1)
                    dve.tensor_tensor(XT.lo[:, :, t * P:(t + 1) * P], bank_view(t),
                                      XT.hi[:, :, t * P:(t + 1) * P].bitcast(F32),
                                      ALU.subtract).then_inc(lo_done, 1)

        @block.scalar
        def _(act):
            if normalise:
                act.wait_ge(var_ready, 1)
                act.activation(moments[:, :, 1], root[:, :], ACT.Sqrt).then_inc(root_ready, 1)
            if XT is not None:
                for t in range(TT):
                    act.wait_ge(turned, t + 1)
                    act.activation(XT.hi[:, :, t * P:(t + 1) * P], bank_view(t), ACT.Copy)\
                       .then_inc(hi_done, 1)

        @block.tensor
        def _(pe):
            if XT is None:
                return
            for t in range(TT):
                if normalise:
                    pe.wait_ge(x_ready, t + 1)
                if t >= 2:
                    pe.wait_ge(lo_done, t - 1)
                for k in range(KT):
                    last = pe.transpose(banks[t % 2][:, k * P:(k + 1) * P], X[:, t, k * P:(k + 1) * P], ident[:, :])
                last.then_inc(turned, 1)


def latent_query_block(nc, XT, LQ, banks, w_lq):
    with ExitStack() as ctx:
        sem = lambda n: ctx.enter_context(nc.semaphore("lq_" + n))
        raw = ctx.enter_context(nc.sbuf_tensor("lq_raw", [P, KT, P], F32))
        W = Pair(ctx, nc, "lq_w", [P, KT, P])
        landed, w_hi, w_ready = sem("landed"), sem("w_hi"), sem("w_ready")
        multiplied, hi_done, lo_done = sem("multiplied"), sem("hi_done"), sem("lo_done")
        block = ctx.enter_context(nc.Block())

        @block.sync
        def _(sp):
            sp.dma_start(raw[:, :, :], w_lq.rearrange("(k p) m -> p k m", p=P)).then_inc(landed, 16)

        @block.vector
        def _(dve):
            dve.wait_ge(landed, 16)
            dve.tensor_copy(W.hi[:, :, :], raw[:, :, :]).then_inc(w_hi, 1)
            dve.wait_ge(w_hi, 1)
            dve.tensor_tensor(W.lo[:, :, :], raw[:, :, :], W.hi[:, :, :].bitcast(F32), ALU.subtract)\
               .then_inc(w_ready, 1)
            for h in range(2):
                dve.wait_ge(hi_done, h + 1)
                at = slice(h * HALF, (h + 1) * HALF)
                dve.tensor_tensor(LQ.lo[:, at], banks[h][:, :], LQ.hi[:, at].bitcast(F32), ALU.subtract)\
                   .then_inc(lo_done, 1)

        @block.scalar
        def _(act):
            for h in range(2):
                act.wait_ge(multiplied, h + 1)
                act.activation(LQ.hi[:, h * HALF:(h + 1) * HALF], banks[h][:, :], ACT.Copy)\
                   .then_inc(hi_done, 1)

        @block.tensor
        def _(pe):
            pe.wait_ge(w_ready, 1)
            for h in range(2):
                for k in range(KT):
                    last = product(pe, banks[h][:, :], W[:, k, :], XT[:, k, h * HALF:(h + 1) * HALF],
                                   k == 0, k == KT - 1)
                last.then_inc(multiplied, 1)


def latent_block(nc, XT, CQ, KC, CV, banks, w_down, cos_d, sin_d):
    N = QL + LAT + ROPE
    with ExitStack() as ctx:
        sb = lambda n, s, d: ctx.enter_context(nc.sbuf_tensor("l_" + n, s, d))
        sem = lambda n: ctx.enter_context(nc.semaphore("l_" + n))
        raw = sb("raw", [P, KT, N], F32)
        cos, sin = sb("cos", [P, SEQ], F32), sb("sin", [P, SEQ], F32)
        straight, crossed = sb("straight", [P, 2, HALF], F32), sb("crossed", [P, 2, HALF], F32)
        W = Pair(ctx, nc, "l_w", [P, KT, N])
        landed, w_hi, w_ready = sem("landed"), sem("w_hi"), sem("w_ready")
        multiplied, hi_done, lo_done = sem("multiplied"), sem("hi_done"), sem("lo_done")
        crossed_done, rotated = sem("crossed_done"), sem("rotated")
        units = [(at, h, rows) for at, rows in ((0, P), (P, QL - P), (QL, P)) for h in range(2)]
        dst = [lambda x, h: x[0][:, 0, h], lambda x, h: x[0][0:QL - P, 1, h], lambda x, h: x[1][:, h]]
        block = ctx.enter_context(nc.Block())

        @block.sync
        def _(sp):
            for d, s in ((raw[:, :, :], w_down.rearrange("(k p) m -> p k m", p=P)), (cos[:, :], cos_d),
                         (sin[:, :], sin_d)):
                sp.dma_start(d, s).then_inc(landed, 16)

        @block.vector
        def _(dve):
            dve.wait_ge(landed, 48)
            dve.tensor_copy(W.hi[:, :, :], raw[:, :, :]).then_inc(w_hi, 1)
            dve.wait_ge(w_hi, 1)
            dve.tensor_tensor(W.lo[:, :, :], raw[:, :, :], W.hi[:, :, :].bitcast(F32), ALU.subtract)\
               .then_inc(w_ready, 1)
            wide = lambda x: x.unsqueeze(1).to_broadcast([x.shape[0], 2, SEQ])
            two = lambda x: x.rearrange("p (s t) -> p s t", s=2)
            for h in range(2):
                dve.wait_ge(multiplied, 5 + h)
                bank, mid = banks[4 + h], LAT + ROPE // 2
                dve.tensor_tensor(two(straight[:, h, :]), two(bank[:, :]), wide(cos[:, :]), ALU.mult)
                dve.tensor_tensor(two(crossed[LAT:mid, h, :]), two(bank[mid:P, :]), wide(sin[mid:P, :]),
                                  ALU.mult)
                dve.tensor_tensor(two(crossed[mid:P, h, :]), two(bank[LAT:mid, :]), wide(sin[LAT:mid, :]),
                                  ALU.mult).then_inc(crossed_done, 1)
                dve.wait_ge(crossed_done, h + 1)
                dve.tensor_tensor(straight[LAT:P, h, :], straight[LAT:P, h, :], crossed[LAT:P, h, :], ALU.add)\
                   .then_inc(rotated, 1)
            for u, (_, h, rows) in enumerate(units):
                dve.wait_ge(hi_done, u + 1)
                at = slice(h * HALF, (h + 1) * HALF)
                hi, lo = (dst[u // 2]((c, k), at) for c, k in ((CQ.hi, KC.hi), (CQ.lo, KC.lo)))
                src = banks[u][0:rows, :] if u < 4 else straight[:, h, :]
                dve.tensor_tensor(lo, src, hi.bitcast(F32), ALU.subtract)
            dve.wait_ge(hi_done, 7)
            dve.tensor_tensor(CV.lo[:, :, :].rearrange("p t r -> p (t r)"), banks[6][:, :],
                              CV.hi[:, :, :].rearrange("p t r -> p (t r)").bitcast(F32), ALU.subtract)

        @block.scalar
        def _(act):
            for u, (_, h, rows) in enumerate(units):
                at = slice(h * HALF, (h + 1) * HALF)
                hi = dst[u // 2]((CQ.hi, KC.hi), at)
                if u < 4:
                    act.wait_ge(multiplied, u + 1)
                else:
                    act.wait_ge(rotated, h + 1)
                act.activation(hi, banks[u][0:rows, :] if u < 4 else straight[:, h, :], ACT.Copy)\
                   .then_inc(hi_done, 1)
            act.wait_ge(multiplied, 7)
            act.activation(CV.hi[:, :, :].rearrange("p t r -> p (t r)"), banks[6][:, :], ACT.Copy)\
               .then_inc(hi_done, 1)

        @block.tensor
        def _(pe):
            pe.wait_ge(w_ready, 1)
            for u, (at, h, rows) in enumerate(units):
                for k in range(KT):
                    last = product(pe, banks[u][0:rows, :], W[:, k, at:at + rows],
                                   XT[:, k, h * HALF:(h + 1) * HALF], k == 0, k == KT - 1)
                last.then_inc(multiplied, 1)
            for t in range(TT):
                for k in range(KT):
                    last = product(pe, banks[6][:, t * LAT:(t + 1) * LAT], XT[:, k, t * P:(t + 1) * P],
                                   W[:, k, QL:QL + LAT], k == 0, k == KT - 1)
            last.then_inc(multiplied, 1)


def l0_pieces(first, last):
    out = [(-1, (kind, 0)) for kind in ("N0", "N1", "R", "UV")] if first else []
    for n, kind, ahead in ((1, "W0", 0), (5, "N0", 1), (7, "W1", 0), (9, "N1", 1), (11, "R", 1), (14, "UV", 1)):
        if not (last and ahead):
            out.append((n, (kind, ahead)))
    return out


def l0_units(first, last):
    out = [("W", -1, 0), ("A", -1, 0), ("A", -1, 1)] if first else []
    for n in range(STEPS):
        j, b = divmod(n, BATCH)
        if j < PER - 1 or not last:
            out += {0: [("W", j, 0)], 1: [("A", j, 0)], 2: [("A", j, 1)], 3: []}[b]
        if j == 0 and not first:
            out += [("O", 0, 2 * b), ("O", 0, 2 * b + 1)]
        if n in (4, 7, 10, 13):
            out.append(("B", (n - 4) // 3, 0))
    return out


def l0_attention_block(nc, X, CQ, KC, CV, ident, banks, w_n, w_r, w_uv, w_o, cos_d, sin_d, mask_d):
    scale = float(np.float32(1.0) / np.sqrt(np.float32(HD + ROPE)))
    with ExitStack() as ctx:
        sb = lambda n, s, d: ctx.enter_context(nc.sbuf_tensor("a0_" + n, s, d))
        sem = lambda n: ctx.enter_context(nc.semaphore("a0_" + n))
        pair = lambda n, s: Pair(ctx, nc, "a0_" + n, s)
        raw = sb("raw", [P, 2, 1024], F32)
        WN = pair("wn", [P, PER, QL + LAT])
        QW = pair("qw", [P, PER, 2, P])
        WUV = pair("wuv", [P, PER, LAT])
        WOUT = pair("wout", [P, PER, D])
        BH = pair("bh", [P, 2, D])
        Q = pair("q", [P, 2, TOK])
        PT = pair("pt", [P, 2, 3 * P])
        OT = pair("ot", [P, 2, TOK])
        cos, sin = sb("cos", [P, SEQ], F32), sb("sin", [P, SEQ], F32)
        mask = sb("mask", [P, SEQ], F32)
        straight = sb("straight", [P, 2, HALF], F32)
        crossed = sb("crossed", [P, HALF], F32)
        probs = sb("probs", [P, 2, 3 * P], F32)
        peak, shift = sb("peak", [P, 2, 2], F32), sb("shift", [P, 2, 2], F32)
        total, share = sb("total", [P, 2, 2], F32), sb("share", [P, 2, 2], F32)
        SA, SB_, TA, _, AV = banks[0:5]
        ring = banks[5:8]

        tables, passed = sem("tables"), {"pool": sem("passed_pool"), "dve": sem("passed_dve")}
        landed = [sem("landed0"), sem("landed1")]
        split_hi, split = sem("split_hi"), sem("split")
        unit_done, ring_free, plain_hi = sem("unit_done"), sem("ring_free"), sem("plain_hi")
        rope_crossed, rope_sum, rope_hi, rope_lo = (sem("rope_crossed"), sem("rope_sum"), sem("rope_hi"),
                                                    sem("rope_lo"))
        scored, peaked, shifted, exped = sem("scored"), sem("peaked"), sem("shifted"), sem("exped")
        shared, scaled, turned = sem("shared"), sem("scaled"), sem("turned")
        pt_hi, pt_lo, applied, ot_hi, ot_lo = (sem("pt_hi"), sem("pt_lo"), sem("applied"), sem("ot_hi"),
                                               sem("ot_lo"))

        calls = [(SA, 0, P), (SB_, P, SEQ)]
        NC = len(calls)
        count = lambda f: len(f(True, False)) + (GROUPS - 2) * len(f(False, False)) + len(f(False, True))
        TOTAL_UNITS, TOTAL_PIECES = count(l0_units), count(l0_pieces)

        def span(kind, first, last, g):
            lists = {"pieces": lambda f, l: [x for _, x in l0_pieces(f, l)], "units": l0_units,
                     "roped": lambda f, l: [u for u in l0_units(f, l) if u[0] == "A"],
                     "plain": lambda f, l: [u for u in l0_units(f, l) if u[0] in "WB"]}[kind]
            n0, n1 = len(lists(True, False)), len(lists(False, False))
            base = 0 if first else n0 + n1 * (g - 1)
            odd = 0 if first else n0
            names = lists(first, last)
            return {x: base + i for i, x in enumerate(names)}, {x: odd + i for i, x in enumerate(names)}

        assert len(l0_pieces(False, False)) % 2 == 0 and len(l0_units(False, False)) % 3 == 0

        def groups(eng, body):
            body(0, True, False)
            with eng.Fori(1, GROUPS - 1) as g:
                body(g, False, False)
            body(GROUPS - 1, False, True)

        def query_cell(x, j, h):
            return x[:, (j + 1) % 2, h * HALF:(h + 1) * HALF]

        def plain_cells(name, bank, x):
            kind, j, _ = name
            if kind == "W":
                j = (j + 1) % PER
                return [(x[0][:, j, 0, 0:LAT], bank[:, 0:LAT]),
                        (x[0][0:QL - P, j, 1, 0:LAT], bank[0:QL - P, LAT:2 * LAT])]
            rows = slice(j % 2 * LAT, (j % 2 + 1) * LAT)
            return [(x[1][rows, j // 2, :], bank[0:LAT, :])]

        def out_cell(x, n):
            j, b = divmod(n % STEPS, BATCH)
            return x[j % 2 * LAT:(j % 2 + 1) * LAT, j // 2, b * SEQ:(b + 1) * SEQ]

        block = ctx.enter_context(nc.Block())

        @block.sync
        def _(sp):
            sp.dma_start(cos[:, :], cos_d).then_inc(tables, 16)
            sp.dma_start(sin[:, :], sin_d).then_inc(tables, 16)
            sp.dma_start(mask[:, :], mask_d).then_inc(tables, 16)

            def body(g, first, last):
                at, place = span("pieces", first, last, g)
                for _, name in l0_pieces(first, last):
                    kind, ahead = name
                    slot = place[name] % 2
                    wait(sp, split, at[name] - 1)
                    src = {"N0": lambda: w_n[bass.ds(2 * (g + ahead), 1)],
                           "N1": lambda: w_n[bass.ds(2 * (g + ahead) + 1, 1)],
                           "R": lambda: w_r[bass.ds(g + ahead, 1)],
                           "UV": lambda: w_uv[bass.ds(g + ahead, 1)],
                           "W0": lambda: w_o[bass.ds(2 * g, 1)],
                           "W1": lambda: w_o[bass.ds(2 * g + 1, 1)]}[kind]()
                    n = src.shape[-1]
                    sp.dma_start(raw[:, slot, 0:n], src.rearrange("a p n -> (a p) n"))\
                      .then_inc(landed[slot], 16)

            groups(sp, body)

        @block.gpsimd
        def _(pool):
            def body(g, first, last):
                at, place = span("pieces", first, last, g)
                roped, roped_place = span("roped", first, last, g)
                number, _ = span("units", first, last, g)

                def split_piece(name):
                    kind, ahead = name
                    slot, index = place[name] % 2, at[name]
                    cell = {"N0": lambda: (WN, lambda x: x[:, 0:2, :]), "N1": lambda: (WN, lambda x: x[:, 2:4, :]),
                            "R": lambda: (QW, lambda x: x[:, :, :, LAT:P]),
                            "UV": lambda: (WUV, lambda x: x[:, :, :]),
                            "W0": lambda: (WOUT, lambda x: x[:, 0:2, :]),
                            "W1": lambda: (WOUT, lambda x: x[:, 2:4, :])}[kind]()
                    hi, lo = cell[1](cell[0].hi), cell[1](cell[0].lo)
                    n = int(np.prod(hi.shape[1:]))
                    src = raw[:, slot, 0:n]
                    src = src.rearrange("p (a b) -> p a b", b=hi.shape[2]) if len(hi.shape) == 3 else \
                        src.rearrange("p (a b c) -> p a b c", b=hi.shape[2], c=hi.shape[3])
                    user = {"N0": ("W", 0, 0), "N1": ("W", 2, 0), "R": ("A", 2, 1), "UV": ("B", 3, 0)}
                    free = number[user[kind]] + 1 if ahead else 0 if first else number[("W", 0, 0)]
                    hold(pool, passed["pool"], (landed[slot], 8 * (index - slot) + 16), (unit_done, free))
                    pool.tensor_scalar(hi, src, 1.0, 1.0, ALU.mult, ALU.mult).then_inc(split_hi, 1)
                    wait(pool, split_hi, index + 1)
                    pool.tensor_tensor(lo, src, hi.bitcast(F32), ALU.subtract).then_inc(split, 1)

                def rope_low(name):
                    _, j, h = name
                    wait(pool, rope_hi, roped[name] + 1)
                    pool.tensor_tensor(query_cell(Q.lo, j, h), straight[:, roped_place[name] % 2, :],
                                       query_cell(Q.hi, j, h).bitcast(F32), ALU.subtract).then_inc(rope_lo, 1)

                def pieces(n):
                    for step, name in l0_pieces(first, last):
                        if step == n:
                            split_piece(name)

                pieces(-1)
                if first:
                    for h in range(2):
                        rope_low(("A", -1, h))
                for n in range(STEPS):
                    j, b = divmod(n, BATCH)
                    if b in (1, 2) and (j < PER - 1 or not last):
                        rope_low(("A", j, b - 1))
                    pieces(n)

            groups(pool, body)

        @block.scalar
        def _(act):
            def body(g, first, last):
                roped, roped_place = span("roped", first, last, g)
                number, bank_of = span("units", first, last, g)

                def rope_high(name):
                    wait(act, rope_sum, roped[name] + 1)
                    act.activation(query_cell(Q.hi, name[1], name[2]), straight[:, roped_place[name] % 2, :],
                                   ACT.Copy).then_inc(rope_hi, 1)

                def plain_high(name):
                    wait(act, unit_done, number[name] + 1)
                    for to, src in plain_cells(name, ring[bank_of[name] % 3], (QW.hi, BH.hi)):
                        ins = act.activation(to, src, ACT.Copy)
                    ins.then_inc(plain_hi, 1)

                def exps(n):
                    wait(act, shifted, STEPS * g + n + 1)
                    for i, (_, col, keys) in enumerate(calls):
                        cell = probs[:, n % 2, col:col + keys]
                        act.activation(cell, cell, ACT.Exp, bias=shift[:, n % 2, i:i + 1], scale=scale,
                                       accum_out=total[:, n % 2, i:i + 1]).then_inc(exped, 1)

                def shares_applied(n):
                    wait(act, shared, STEPS * g + n + 1)
                    for i, (_, col, keys) in enumerate(calls):
                        cell = probs[:, n % 2, col:col + keys]
                        ins = act.activation(cell, cell, ACT.Copy, scale=share[:, n % 2, i:i + 1])
                    ins.then_inc(scaled, 1)

                def probs_high(n):
                    wait(act, turned, STEPS * g + n + 1)
                    wait(act, applied, STEPS * g + n - 1)
                    act.activation(PT.hi[:, n % 2, :], TA[:, 0:3 * P], ACT.Copy).then_inc(pt_hi, 1)

                def out_high(n):
                    wait(act, applied, STEPS * g + n + 1)
                    act.activation(out_cell(OT.hi, n), AV[0:LAT, 0:SEQ], ACT.Copy).then_inc(ot_hi, 1)

                if first:
                    plain_high(("W", -1, 0))
                    for h in range(2):
                        rope_high(("A", -1, h))
                for n in range(STEPS):
                    j, b = divmod(n, BATCH)
                    exps(n)
                    if j < PER - 1 or not last:
                        if b == 0:
                            plain_high(("W", j, 0))
                        if b in (1, 2):
                            rope_high(("A", j, b - 1))
                    if not (first and n == 0):
                        probs_high(n - 1)
                    shares_applied(n)
                    if not (first and n < 2):
                        out_high(n - 2)
                    if n in (4, 7, 10, 13):
                        plain_high(("B", (n - 4) // 3, 0))
                if last:
                    probs_high(STEPS - 1)
                    out_high(STEPS - 2)
                    out_high(STEPS - 1)

            groups(act, body)

        @block.tensor
        def _(pe):
            def output(bank, t, done, free):
                wait(pe, ring_free, free)
                wait(pe, ot_lo, done)
                for i in range(2):
                    last_ = product(pe, bank[:, :], OT[:, i, t * P:(t + 1) * P], BH[:, i, :], i == 0, i == 1)
                last_.then_inc(unit_done, 1)

            def body(g, first, last):
                number, bank_of = span("units", first, last, g)
                pieces, _ = span("pieces", first, last, g)
                roped, _ = span("roped", first, last, g)

                def open_unit(name, after=None):
                    late = after is not None and bank_of[after] + 1 > bank_of[name] - 2
                    wait(pe, ring_free, number[after] + 1 if late else number[name] - 2)
                    return ring[bank_of[name] % 3]

                def piece_ready(kind, j):
                    ahead = j // PER
                    if (kind, ahead) in pieces:
                        count_ = pieces[(kind, ahead)] + 1
                    else:
                        names = [x for _, x in l0_pieces(False, False)]
                        count_ = pieces[names[0]] - (len(names) - names.index((kind, 1))) + 1
                    wait(pe, split, count_)

                def absorb(name):
                    bank = open_unit(name)
                    j = name[1] + 1
                    piece_ready("N0" if j % PER < 2 else "N1", j)
                    j %= PER
                    product(pe, bank[:, 0:LAT], WN[:, j, 0:P], WN[:, j, QL:QL + LAT], True, True)
                    product(pe, bank[0:QL - P, LAT:2 * LAT], WN[:, j, P:QL], WN[:, j, QL:QL + LAT], True, True)\
                        .then_inc(unit_done, 1)

                def queries(name):
                    _, j, h = name
                    bank = open_unit(name, ("W", j, 0))
                    piece_ready("R", j + 1)
                    j = (j + 1) % PER
                    at = slice(h * HALF, (h + 1) * HALF)
                    product(pe, bank[:, :], QW[:, j, 0, :], CQ[:, 0, at], True, False)
                    product(pe, bank[:, :], QW[0:QL - P, j, 1, :], CQ[0:QL - P, 1, at], False, True)\
                        .then_inc(unit_done, 1)

                def output_weights(name):
                    bank = open_unit(name)
                    j = name[1]
                    piece_ready("W0" if j < 2 else "W1", 0)
                    product(pe, bank[0:LAT, :], WUV[:, j, :], WOUT[:, j, :], True, True).then_inc(unit_done, 1)

                def scores(n):
                    j, b = divmod(n, BATCH)
                    if b == 0:
                        name = ("A", j - 1, 1)
                        wait(pe, rope_lo, roped[name] + 1 if name in roped else roped[("A", 0, 0)])
                    wait(pe, peaked, STEPS * g + n)
                    for r, (bank, _, keys) in enumerate(calls):
                        rows = slice(b * SEQ + r * P, b * SEQ + (r + 1) * P)
                        last_ = product(pe, bank[:, 0:keys], Q[:, j % 2, rows], KC[:, b * SEQ:b * SEQ + keys],
                                        True, True)
                    last_.then_inc(scored, 1)

                def turn(n):
                    wait(pe, scaled, STEPS * g + n + 1)
                    wait(pe, pt_lo, STEPS * g + n)
                    for i in range(3):
                        last_ = pe.transpose(TA[:, i * P:(i + 1) * P], probs[:, n % 2, i * P:(i + 1) * P],
                                             ident[:, :])
                    last_.then_inc(turned, 1)

                def apply(n):
                    b = n % BATCH
                    wait(pe, pt_lo, STEPS * g + n + 1)
                    wait(pe, ot_lo, STEPS * g + n)
                    product(pe, AV[0:LAT, 0:SEQ], CV[:, 2 * b, :], PT[:, n % 2, 0:SEQ], True, False)
                    product(pe, AV[0:LAT, P:SEQ], CV[:, 2 * b + 1, :], PT[:, n % 2, SEQ:3 * P], False, True)\
                        .then_inc(applied, 1)

                if first:
                    absorb(("W", -1, 0))
                    for h in range(2):
                        queries(("A", -1, h))
                for n in range(STEPS):
                    j, b = divmod(n, BATCH)
                    scores(n)
                    if j < PER - 1 or not last:
                        if b == 0:
                            absorb(("W", j, 0))
                        if b in (1, 2):
                            queries(("A", j, b - 1))
                    if not (first and n == 0):
                        turn(n - 1)
                    if j == 0 and not first:
                        for t in (2 * b, 2 * b + 1):
                            name = ("O", 0, t)
                            output(ring[bank_of[name] % 3], t, STEPS * (g - 1) + BATCH * (PER - 1) + b + 1,
                                   number[name] - 2 if t else number[("W", 0, 0)])
                    if not (first and n < 2):
                        apply(n - 2)
                    if n in (4, 7, 10, 13):
                        output_weights(("B", (n - 4) // 3, 0))
                if last:
                    turn(STEPS - 1)
                    apply(STEPS - 2)
                    apply(STEPS - 1)

            groups(pe, body)
            wait(pe, ring_free, TOTAL_UNITS)
            for t in range(TT):
                output(ring[(TOTAL_UNITS + t) % 3], t, STEPS * (GROUPS - 1) + BATCH * (PER - 1) + t // 2 + 1,
                       TOTAL_UNITS + t - 2)

        @block.vector
        def _(dve):
            dve.wait_ge(tables, 48)
            wide = lambda x: x.unsqueeze(1).to_broadcast([x.shape[0], 2, SEQ])
            two = lambda x: x.rearrange("p (s t) -> p s t", s=2)
            mid = LAT + ROPE // 2

            def add_output(index, bank, t):
                wait(dve, unit_done, index + 1)
                dve.tensor_tensor(X[:, t, :], bank[:, :], X[:, t, :], ALU.add).then_inc(ring_free, 1)

            def body(g, first, last):
                number, bank_of = span("units", first, last, g)
                roped, roped_place = span("roped", first, last, g)
                plain, _ = span("plain", first, last, g)

                def rotate(name):
                    r, bank = roped[name], ring[bank_of[name] % 3]
                    row = straight[:, roped_place[name] % 2, :]
                    wait(dve, unit_done, number[name] + 1)
                    wait(dve, rope_lo, r - 1)
                    dve.tensor_tensor(two(row), two(bank[:, :]), wide(cos[:, :]), ALU.mult)
                    wait(dve, rope_sum, r)
                    dve.tensor_tensor(two(crossed[LAT:mid, :]), two(bank[mid:P, :]), wide(sin[mid:P, :]), ALU.mult)
                    dve.tensor_tensor(two(crossed[mid:P, :]), two(bank[LAT:mid, :]), wide(sin[LAT:mid, :]),
                                      ALU.mult).then_inc(ring_free, 1)
                    wait(dve, ring_free, number[name] + 1)
                    dve.tensor_tensor(row[LAT:P, :], row[LAT:P, :], crossed[LAT:P, :], ALU.add)\
                       .then_inc(rope_sum, 1)

                def plain_low(name):
                    wait(dve, plain_hi, plain[name] + 1)
                    bank = ring[bank_of[name] % 3]
                    for (to, src), (high, _) in zip(plain_cells(name, bank, (QW.lo, BH.lo)),
                                                    plain_cells(name, bank, (QW.hi, BH.hi))):
                        ins = dve.tensor_tensor(to, src, high.bitcast(F32), ALU.subtract)
                    ins.then_inc(ring_free, 1)

                def peaks(n):
                    hold(dve, passed["dve"], (scored, STEPS * g + n + 1), (turned, STEPS * g + n - 1))
                    for i, (bank, col, keys) in enumerate(calls):
                        ins = dve.tensor_tensor_reduce(
                            out=probs[:, n % 2, col:col + keys], in0=bank[:, 0:keys],
                            in1=mask[:, SEQ - keys:SEQ], scale=1.0, scalar=NEG, op0=ALU.add, op1=ALU.max,
                            accum_out=peak[:, n % 2, i:i + 1])
                    ins.then_inc(peaked, 1)
                    wait(dve, peaked, STEPS * g + n + 1)
                    dve.tensor_scalar(shift[:, n % 2, :], peak[:, n % 2, :], -scale, None, ALU.mult)\
                       .then_inc(shifted, 1)

                def shares(n):
                    wait(dve, exped, NC * (STEPS * g + n + 1))
                    dve.reciprocal(share[:, n % 2, :], total[:, n % 2, :]).then_inc(shared, 1)

                def probs_low(n):
                    wait(dve, pt_hi, STEPS * g + n + 1)
                    dve.tensor_tensor(PT.lo[:, n % 2, :], TA[:, 0:3 * P], PT.hi[:, n % 2, :].bitcast(F32),
                                      ALU.subtract).then_inc(pt_lo, 1)

                def out_low(n):
                    wait(dve, ot_hi, STEPS * g + n + 1)
                    dve.tensor_tensor(out_cell(OT.lo, n), AV[0:LAT, 0:SEQ], out_cell(OT.hi, n).bitcast(F32),
                                      ALU.subtract).then_inc(ot_lo, 1)

                if first:
                    plain_low(("W", -1, 0))
                    for h in range(2):
                        rotate(("A", -1, h))
                for n in range(STEPS):
                    j, b = divmod(n, BATCH)
                    peaks(n)
                    if j < PER - 1 or not last:
                        if b == 0:
                            plain_low(("W", j, 0))
                        if b in (1, 2):
                            rotate(("A", j, b - 1))
                    shares(n)
                    if not (first and n == 0):
                        probs_low(n - 1)
                    if j == 0 and not first:
                        for t in (2 * b, 2 * b + 1):
                            name = ("O", 0, t)
                            add_output(number[name], ring[bank_of[name] % 3], t)
                    if not (first and n < 2):
                        out_low(n - 2)
                    if n in (4, 7, 10, 13):
                        plain_low(("B", (n - 4) // 3, 0))
                if last:
                    probs_low(STEPS - 1)
                    out_low(STEPS - 2)
                    out_low(STEPS - 1)

            groups(dve, body)
            for t in range(TT):
                add_output(TOTAL_UNITS + t, ring[(TOTAL_UNITS + t) % 3], t)


def l1_pieces(first, last):
    out = []
    if first:
        out += [(-1, ("Q", 0)), (-1, ("LK", 0)), (-1, ("KV", 0)), (-1, ("LVa", 0)), (-1, ("Q", 1))]
    for j in range(PER):
        for b in range(BATCH):
            n = 4 * j + b
            if n == 4:
                out.append((n, ("LVb", 0)))
            if b == 1:
                out.append((n, ("WO", j)))
            if b == 3 and (j < 2 or not last):
                out.append((n, ("Q", j + 2)))
            if n == 12 and not last:
                out.append((n, ("LK", PER)))
            if n == 13 and not last:
                out.append((n, ("LVa", PER)))
            if n == 10 and not last:
                out.append((n, ("KV", PER)))
    return out


MADE = ((0,), (1,), (2, 3), ())


def l1_units(first, last):
    out = []
    if first:
        out += [("A", -1, b) for b in range(4)]
    out += [("K", 0, 0), ("K", 0, 1)]
    for j in range(PER):
        for b in range(BATCH):
            n = 4 * j + b
            turn = [("O", j, 2 * b), ("O", j, 2 * b + 1)] if (j or not first) else []
            own = [("A", j, i) for i in MADE[b]] if (j < PER - 1 or not last) else []
            out += turn + own if n == 0 else own + turn
            if n == 1:
                out += [("V", 0, 0), ("V", 0, 1)] + [("LVa", 0, i) for i in range(4)]
            if n == 9:
                out += [("LVb", 0, i) for i in range(4)]
    return out


def l1_attention_block(nc, X, XT, LQ, ident, banks, w_q, w_lk, w_kv, w_lv, w_o, cos_d, sin_d, mask_d):
    NP = 2
    scale = float(np.float32(1.0) / np.sqrt(np.float32(HD)))
    with ExitStack() as ctx:
        sb = lambda n, s, d: ctx.enter_context(nc.sbuf_tensor("a1_" + n, s, d))
        sem = lambda n: ctx.enter_context(nc.semaphore("a1_" + n))
        pair = lambda n, s: Pair(ctx, nc, "a1_" + n, s)
        raw = sb("raw", [P, 2, 1024], F32)
        WQ = pair("wq", [P, KT, P])
        WLK = pair("wlk", [P, PER, P])
        WKV = pair("wkv", [P, 2, KT, P])
        WLV = pair("wlv", [P, KT, 2, P])
        WO = pair("wo", [P, 2, 2, D])
        KK = pair("kk", [P, 3, TOK])
        Q = pair("q", [P, 2, TOK])
        V = pair("v", [P, TT, P])
        LV = pair("lv", [P, TT, 2, P])
        PT = pair("pt", [P, NP, 3 * P])
        OT = pair("ot", [P, NP, TOK])
        cos, sin = sb("cos", [P, SEQ], F32), sb("sin", [P, SEQ], F32)
        mask = sb("mask", [P, SEQ], F32)
        straight = sb("straight", [P, 2, HALF], F32)
        crossed = sb("crossed", [P, HALF], F32)
        probs = sb("probs", [P, 2, NP * 3 * P], F32)
        peak = sb("peak", [P, 2, 4], F32)
        shift = sb("shift", [P, 2, 4], F32)
        total = sb("total", [P, 2, 4], F32)
        share = sb("share", [P, 2, 4], F32)
        SA, SB_, TA, TB, AV = banks[0:5]
        ring = banks[5:8]

        tables, passed = sem("tables"), {"pool": sem("passed_pool"), "dve": sem("passed_dve")}
        landed = [sem("landed0"), sem("landed1")]
        split_hi, split = sem("split_hi"), sem("split")
        unit_done, ring_free = sem("unit_done"), sem("ring_free")
        v_hi = sem("v_hi")
        rope_crossed, rope_sum, rope_hi, rope_lo = (sem("rope_crossed"), sem("rope_sum"), sem("rope_hi"),
                                                    sem("rope_lo"))
        scored, peaked, shifted, exped = sem("scored"), sem("peaked"), sem("shifted"), sem("exped")
        shared, scaled, turned = sem("shared"), sem("scaled"), sem("turned")
        pt_hi, pt_lo, applied, ot_hi, ot_lo = (sem("pt_hi"), sem("pt_lo"), sem("applied"), sem("ot_hi"),
                                               sem("ot_lo"))

        calls = []
        for p in range(NP):
            calls.append((0, p, SA, p * P, p * P, P))
            calls.append((1, p, SB_, p * SEQ, NP * P + p * SEQ, SEQ))
        NC = len(calls)

        def span(kind, first, last, g):
            if kind == "pieces":
                names, n0, n1 = [x for _, x in l1_pieces(first, last)], len(l1_pieces(True, False)), \
                    len(l1_pieces(False, False))
            elif kind == "units":
                names, n0, n1 = l1_units(first, last), len(l1_units(True, False)), len(l1_units(False, False))
            else:
                keep = lambda f, l: [u for u in l1_units(f, l) if u[0] in "AK"]
                if kind == "plain":
                    keep = lambda f, l: [u for u in l1_units(f, l) if u[0] in ("V", "LVa", "LVb")]
                names, n0, n1 = keep(first, last), len(keep(True, False)), len(keep(False, False))
            base = 0 if first else n0 + n1 * (g - 1)
            odd = 0 if first else n0
            return {x: base + i for i, x in enumerate(names)}, {x: odd + i for i, x in enumerate(names)}

        assert len(l1_pieces(False, False)) % 2 == 0 and len(l1_units(False, False)) % 3 == 0

        count = lambda f: len(f(True, False)) + (GROUPS - 2) * len(f(False, False)) + len(f(False, True))
        TOTAL_UNITS, TOTAL_PIECES = count(l1_units), count(l1_pieces)

        def groups(eng, body):
            body(0, True, False)
            with eng.Fori(1, GROUPS - 1) as g:
                body(g, False, False)
            body(GROUPS - 1, False, True)

        def destination(kind, j, b):
            class Part:
                pass
            to = Part()
            h = b if kind == "K" else b % 2
            at = slice(h * HALF, (h + 1) * HALF)
            if kind == "K":
                to.hi, to.lo = KK.hi[:, 0, at], KK.lo[:, 0, at]
            elif b < 2:
                to.hi, to.lo = Q.hi[:, (j + 1) % 2, at], Q.lo[:, (j + 1) % 2, at]
            else:
                to.hi, to.lo = KK.hi[:, 1 + (j + 1) % 2, at], KK.lo[:, 1 + (j + 1) % 2, at]
            return to

        def plain_cell(name, x):
            kind, _, i = name
            if kind == "V":
                return x[0][:, 4 * i:4 * i + 4, :]
            return x[1][:, 2 * i:2 * i + 2, :, :]

        def plain_bank(name, bank):
            if name[0] == "V":
                return bank[:, :].rearrange("p (t d) -> p t d", t=4)
            return bank[:, :].rearrange("p (t h d) -> p t h d", t=2, h=2)

        block = ctx.enter_context(nc.Block())

        @block.sync
        def _(sp):
            sp.dma_start(cos[:, :], cos_d).then_inc(tables, 16)
            sp.dma_start(sin[:, :], sin_d).then_inc(tables, 16)
            sp.dma_start(mask[:, :], mask_d).then_inc(tables, 16)

            def body(g, first, last):
                at, place = span("pieces", first, last, g)
                for _, name in l1_pieces(first, last):
                    kind, j = name
                    slot = place[name] % 2
                    wait(sp, split, at[name] - 1)
                    src = {"Q": lambda: w_q[bass.ds(PER * g + j, 1)],
                           "LK": lambda: w_lk[bass.ds(g + j // PER, 1)],
                           "KV": lambda: w_kv[bass.ds(g + j // PER, 1)],
                           "LVa": lambda: w_lv[bass.ds(2 * (g + j // PER), 1)],
                           "LVb": lambda: w_lv[bass.ds(2 * g + 1, 1)],
                           "WO": lambda: w_o[bass.ds(PER * g + j, 1)]}[kind]()
                    n = src.shape[-1]
                    sp.dma_start(raw[:, slot, 0:n], src.rearrange("a p n -> (a p) n"))\
                      .then_inc(landed[slot], 16)

            groups(sp, body)

        @block.gpsimd
        def _(pool):
            def split_piece(name, at, place, units):
                kind, j = name
                slot = place[name] % 2
                n = {"Q": 512, "LK": 512}.get(kind, 1024)
                dst = {"Q": lambda x: x[:, :, :], "LK": lambda x: x[:, :, :], "KV": lambda x: x[:, :, :, :],
                       "LVa": lambda x: x[:, :, :, :], "LVb": lambda x: x[:, :, :, :],
                       "WO": lambda x: x[:, j % 2, :, :]}[kind]
                W = {"Q": WQ, "LK": WLK, "KV": WKV, "LVa": WLV, "LVb": WLV, "WO": WO}[kind]
                hi, lo = dst(W.hi), dst(W.lo)
                shape = {3: "p (a b) -> p a b", 4: "p (a b c) -> p a b c"}[len(hi.shape)]
                sizes = {"b": hi.shape[2]} if len(hi.shape) == 3 else {"b": hi.shape[2], "c": hi.shape[3]}
                src = raw[:, slot, 0:n].rearrange(shape, **sizes)
                index = at[name]
                free = units(name)
                hold(pool, passed["pool"], (landed[slot], 8 * (index - slot) + 16),
                     (unit_done, 0 if free is None else free))
                pool.tensor_scalar(hi, src, 1.0, 1.0, ALU.mult, ALU.mult).then_inc(split_hi, 1)
                wait(pool, split_hi, index + 1)
                pool.tensor_tensor(lo, src, hi.bitcast(F32), ALU.subtract).then_inc(split, 1)

            def rope_low(name, roped, place):
                kind, j, b = name
                h = b if kind == "K" else b % 2
                to = destination(kind, j, b)
                wait(pool, rope_hi, roped[name] + 1)
                pool.tensor_tensor(to.lo, straight[:, place[name] % 2, :], to.hi.bitcast(F32), ALU.subtract)\
                    .then_inc(rope_lo, 1)

            def body(g, first, last):
                at, place = span("pieces", first, last, g)
                roped, roped_place = span("roped", first, last, g)
                number, _ = span("units", first, last, g)

                def free(name):
                    kind, j = name
                    if kind == "Q" and not (first and j == 0):
                        return number[("A", j - 2, 1)] + 1
                    if kind == "LK" and j:
                        return number[("A", 2, 3)] + 1
                    if kind == "LVb":
                        return number[("LVa", 0, 3)] + 1
                    if kind == "LVa" and j:
                        return number[("LVb", 0, 3)] + 1
                    if kind == "KV" and j:
                        return number[("V", 0, 1)] + 1
                    if kind == "WO":
                        if first and j < 2:
                            return None
                        return number[("O", j - 1, 7)] + 1 if j else number[("K", 0, 0)]
                    return None

                def pieces(n):
                    for step, name in l1_pieces(first, last):
                        if step == n:
                            split_piece(name, at, place, free)

                pieces(-1)
                if first:
                    for b in range(4):
                        rope_low(("A", -1, b), roped, roped_place)
                for h in range(2):
                    rope_low(("K", 0, h), roped, roped_place)
                for n in range(STEPS):
                    j, b = divmod(n, BATCH)
                    if j < PER - 1 or not last:
                        for i in MADE[b]:
                            rope_low(("A", j, i), roped, roped_place)
                    pieces(n)

            groups(pool, body)

        @block.scalar
        def _(act):
            def body(g, first, last):
                roped, roped_place = span("roped", first, last, g)
                number, bank_of = span("units", first, last, g)

                def rope_high(name):
                    to = destination(*name)
                    wait(act, rope_sum, roped[name] + 1)
                    act.activation(to.hi, straight[:, roped_place[name] % 2, :], ACT.Copy)\
                       .then_inc(rope_hi, 1)

                def plain_high(name):
                    wait(act, unit_done, number[name] + 1)
                    act.activation(plain_cell(name, (V.hi, LV.hi)),
                                   plain_bank(name, ring[bank_of[name] % 3]), ACT.Copy).then_inc(v_hi, 1)

                def exps(n):
                    wait(act, shifted, STEPS * g + n + 1)
                    for i, (r, p, _, _, col, keys) in enumerate(calls):
                        cell = probs[:, n % 2, col:col + keys]
                        act.activation(cell, cell, ACT.Exp, bias=shift[:, n % 2, i:i + 1], scale=scale,
                                       accum_out=total[:, n % 2, i:i + 1]).then_inc(exped, 1)

                def shares_applied(n):
                    wait(act, shared, STEPS * g + n + 1)
                    for i, (_, _, _, _, col, keys) in enumerate(calls):
                        cell = probs[:, n % 2, col:col + keys]
                        ins = act.activation(cell, cell, ACT.Copy, scale=share[:, n % 2, i:i + 1])
                    ins.then_inc(scaled, 1)

                def probs_high(n):
                    wait(act, turned, STEPS * g + n + 1)
                    wait(act, applied, STEPS * g + n)
                    for p, bank in enumerate((TA, TB)):
                        ins = act.activation(PT.hi[:, p, :], bank[:, 0:3 * P], ACT.Copy)
                    ins.then_inc(pt_hi, 1)

                def out_high(n):
                    b = n % BATCH
                    wait(act, applied, STEPS * g + n + 1)
                    act.activation(OT.hi[:, :, b * SEQ:(b + 1) * SEQ],
                                   AV[:, :].rearrange("p (a s) -> p a s", a=NP), ACT.Copy)\
                       .then_inc(ot_hi, 1)

                if first:
                    for b in range(4):
                        rope_high(("A", -1, b))
                for h in range(2):
                    rope_high(("K", 0, h))
                for n in range(STEPS):
                    j, b = divmod(n, BATCH)
                    if n == 0:
                        if not first:
                            out_high(-2)
                            probs_high(-1)
                        rope_high(("A", 0, 0))
                        exps(0)
                        shares_applied(0)
                        continue
                    if not (first and n < 2):
                        out_high(n - 2)
                    exps(n)
                    probs_high(n - 1)
                    shares_applied(n)
                    if j < PER - 1 or not last:
                        for i in MADE[b]:
                            rope_high(("A", j, i))
                    if n == 1:
                        for i in range(2):
                            plain_high(("V", 0, i))
                        for i in range(4):
                            plain_high(("LVa", 0, i))
                    if n == 9:
                        for i in range(4):
                            plain_high(("LVb", 0, i))
                if last:
                    out_high(STEPS - 2)
                    probs_high(STEPS - 1)
                    out_high(STEPS - 1)

            groups(act, body)

        @block.tensor
        def _(pe):
            def body(g, first, last):
                number, bank_of = span("units", first, last, g)
                pieces, _ = span("pieces", first, last, g)
                roped, _ = span("roped", first, last, g)

                def open_unit(name):
                    bank = ring[bank_of[name] % 3]
                    wait(pe, ring_free, number[name] - 2)
                    return bank

                def piece_ready(name):
                    if name in pieces:
                        count = pieces[name] + 1
                    else:
                        names = [x for _, x in l1_pieces(False, False)]
                        kind, j = name
                        count = pieces[names[0]] - (len(names) - names.index((kind, j + PER))) + 1
                    wait(pe, split, count)

                def project(name):
                    kind, j, b = name
                    bank = open_unit(name)
                    h = b if kind == "K" else b % 2
                    at = slice(h * HALF, (h + 1) * HALF)
                    if kind == "A" and b >= 2:
                        if j in (-1, PER - 1):
                            piece_ready(("LK", j + 1))
                        last_ = product(pe, bank[:, :], WLK[:, (j + 1) % PER, :], LQ[:, at], True, True)
                    else:
                        piece_ready(("KV", 0) if kind == "K" else ("Q", j + 1))
                        for k in range(KT):
                            w = WKV[:, 0, k, :] if kind == "K" else WQ[:, k, :]
                            last_ = product(pe, bank[:, :], w, XT[:, k, at], k == 0, k == KT - 1)
                    last_.then_inc(unit_done, 1)

                def values(name):
                    kind, _, i = name
                    bank = open_unit(name)
                    out = plain_bank(name, bank)
                    if i == 0 and kind != "V":
                        piece_ready((kind, 0))
                    tiles = 4 if kind == "V" else 2
                    for t in range(tiles):
                        at = slice((tiles * i + t) * P, (tiles * i + t + 1) * P)
                        for k in range(KT):
                            w = WKV[:, 1, k, :] if kind == "V" else WLV[:, k, :, :]
                            o = out[:, t, :] if kind == "V" else out[:, t, :, :]
                            last_ = product(pe, o, XT[:, k, at], w, k == 0, k == KT - 1)
                    last_.then_inc(unit_done, 1)

                def scores(n):
                    j, b = divmod(n, BATCH)
                    if b == 0:
                        need = ("K", 0, 1) if j == 0 else ("A", j - 1, 3)
                        wait(pe, rope_lo, roped[need] + 1)
                    wait(pe, peaked, STEPS * g + n)
                    keys = slice(0, 3, 2) if j % 2 else slice(0, 2)
                    for r, bank in ((0, SA), (1, SB_)):
                        rows = slice(b * SEQ + r * P, b * SEQ + (r + 1) * P)
                        cols = slice(b * SEQ, b * SEQ + (r + 1) * P)
                        out = bank[:, 0:NP * (r + 1) * P].rearrange("p (a t) -> p a t", a=NP)
                        last_ = product(pe, out, Q[:, j % 2, rows], KK[:, keys, cols], True, True)
                    last_.then_inc(scored, 1)

                def turn(n):
                    wait(pe, scaled, STEPS * g + n + 1)
                    wait(pe, pt_lo, STEPS * g + n)
                    for p, bank in enumerate((TA, TB)):
                        for i, col in enumerate((p * P, NP * P + p * SEQ, NP * P + p * SEQ + P)):
                            last_ = pe.transpose(bank[:, i * P:(i + 1) * P], probs[:, n % 2, col:col + P],
                                                 ident[:, :])
                    last_.then_inc(turned, 1)

                def apply(n):
                    b, j = n % BATCH, (n // BATCH) % PER
                    wait(pe, pt_lo, STEPS * g + n + 1)
                    wait(pe, ot_lo, STEPS * g + n)
                    if j == 0 and b == 0:
                        wait(pe, ring_free, number[("LVa", 0, 3)] + 1)
                    if j == 2 and b == 0:
                        wait(pe, ring_free, number[("LVb", 0, 3)] + 1)
                    for p in range(NP):
                        for t in range(2):
                            v = V[:, 2 * b + t, :] if p == 0 else LV[:, 2 * b + t, j % 2, :]
                            out = AV[:, p * SEQ + t * P:(p + 1) * SEQ]
                            last_ = product(pe, out, v,
                                            PT[:, p, 0:SEQ] if t == 0 else PT[:, p, SEQ:3 * P],
                                            t == 0, t == 1)
                    last_.then_inc(applied, 1)

                def output(name):
                    _, j, t = name
                    bank = open_unit(name)
                    wait(pe, ot_lo, STEPS * g + BATCH * (j - 1) + t // 2 + 1)
                    if t == 0:
                        piece_ready(("WO", j - 1))
                    for p in range(NP):
                        last_ = product(pe, bank[:, :], OT[:, p, t * P:(t + 1) * P],
                                        WO[:, (j - 1) % 2, p, :], p == 0, p == NP - 1)
                    last_.then_inc(unit_done, 1)

                if first:
                    for b in range(4):
                        project(("A", -1, b))
                for h in range(2):
                    project(("K", 0, h))
                for n in range(STEPS):
                    j, b = divmod(n, BATCH)
                    outs = [("O", j, 2 * b), ("O", j, 2 * b + 1)] if (j or not first) else []
                    own = j < PER - 1 or not last
                    if n == 0:
                        if not first:
                            apply(-2)
                            turn(-1)
                            for o in outs:
                                output(o)
                        project(("A", 0, 0))
                        scores(0)
                        continue
                    scores(n)
                    if not (first and n < 2):
                        apply(n - 2)
                    turn(n - 1)
                    if own:
                        for i in MADE[b]:
                            project(("A", j, i))
                    for o in outs:
                        output(o)
                    if n == 1:
                        for i in range(2):
                            values(("V", 0, i))
                        for i in range(4):
                            values(("LVa", 0, i))
                    if n == 9:
                        for i in range(4):
                            values(("LVb", 0, i))
                if last:
                    apply(STEPS - 2)
                    turn(STEPS - 1)
                    apply(STEPS - 1)
                    for t in range(TT):
                        tail_output(g, number, t, pieces)

            def tail_output(g, number, t, pieces):
                index = TOTAL_UNITS + t
                wait(pe, ring_free, index - 2)
                wait(pe, ot_lo, STEPS * (GROUPS - 1) + BATCH * (PER - 1) + t // 2 + 1)
                if t == 0:
                    wait(pe, split, TOTAL_PIECES)
                bank = ring[index % 3]
                for p in range(NP):
                    last_ = product(pe, bank[:, :], OT[:, p, t * P:(t + 1) * P], WO[:, (PER - 1) % 2, p, :],
                                    p == 0, p == NP - 1)
                last_.then_inc(unit_done, 1)

            groups(pe, body)

        @block.vector
        def _(dve):
            dve.wait_ge(tables, 48)

            def add_output(index, bank_index, t):
                wait(dve, unit_done, index + 1)
                dve.tensor_tensor(X[:, t, :], ring[bank_index % 3][:, :], X[:, t, :], ALU.add)\
                   .then_inc(ring_free, 1)

            def body(g, first, last):
                number, bank_of = span("units", first, last, g)
                roped, roped_place = span("roped", first, last, g)
                plain, _ = span("plain", first, last, g)

                def rotate(name):
                    r = roped[name]
                    bank = ring[bank_of[name] % 3]
                    row = straight[:, roped_place[name] % 2, :]
                    wide = lambda x: x.unsqueeze(1).to_broadcast([x.shape[0], 2, SEQ])
                    two = lambda x: x.rearrange("p (s t) -> p s t", s=2)
                    wait(dve, unit_done, number[name] + 1)
                    wait(dve, rope_lo, r - 1)
                    dve.tensor_tensor(two(row), two(bank[:, :]), wide(cos[:, :]), ALU.mult)
                    wait(dve, rope_sum, r)
                    dve.tensor_tensor(two(crossed[0:64, :]), two(bank[64:P, :]), wide(sin[64:P, :]), ALU.mult)
                    dve.tensor_tensor(two(crossed[64:P, :]), two(bank[0:64, :]), wide(sin[0:64, :]), ALU.mult)\
                       .then_inc(ring_free, 1)
                    wait(dve, ring_free, number[name] + 1)
                    dve.tensor_tensor(row, row, crossed[:, :], ALU.add).then_inc(rope_sum, 1)

                def plain_low(name):
                    wait(dve, v_hi, plain[name] + 1)
                    dve.tensor_tensor(plain_cell(name, (V.lo, LV.lo)), plain_bank(name, ring[bank_of[name] % 3]),
                                      plain_cell(name, (V.hi, LV.hi)).bitcast(F32), ALU.subtract)\
                       .then_inc(ring_free, 1)

                def peaks(n):
                    hold(dve, passed["dve"], (scored, STEPS * g + n + 1), (turned, STEPS * g + n - 1))
                    for i, (r, p, bank, at, col, keys) in enumerate(calls):
                        ins = dve.tensor_tensor_reduce(
                            out=probs[:, n % 2, col:col + keys], in0=bank[:, at:at + keys],
                            in1=mask[:, SEQ - keys:SEQ], scale=1.0, scalar=NEG, op0=ALU.add, op1=ALU.max,
                            accum_out=peak[:, n % 2, i:i + 1])
                    ins.then_inc(peaked, 1)
                    wait(dve, peaked, STEPS * g + n + 1)
                    dve.tensor_scalar(shift[:, n % 2, :], peak[:, n % 2, :], -scale, None, ALU.mult)\
                       .then_inc(shifted, 1)

                def shares(n):
                    wait(dve, exped, NC * (STEPS * g + n + 1))
                    dve.reciprocal(share[:, n % 2, :], total[:, n % 2, :]).then_inc(shared, 1)

                def probs_low(n):
                    wait(dve, pt_hi, STEPS * g + n + 1)
                    for p, bank in enumerate((TA, TB)):
                        ins = dve.tensor_tensor(PT.lo[:, p, :], bank[:, 0:3 * P],
                                                PT.hi[:, p, :].bitcast(F32), ALU.subtract)
                    ins.then_inc(pt_lo, 1)

                def out_low(n):
                    b = n % BATCH
                    at = slice(b * SEQ, (b + 1) * SEQ)
                    wait(dve, ot_hi, STEPS * g + n + 1)
                    dve.tensor_tensor(OT.lo[:, :, at], AV[:, :].rearrange("p (a s) -> p a s", a=NP),
                                      OT.hi[:, :, at].bitcast(F32), ALU.subtract).then_inc(ot_lo, 1)

                if first:
                    for b in range(4):
                        rotate(("A", -1, b))
                for h in range(2):
                    rotate(("K", 0, h))
                for n in range(STEPS):
                    j, b = divmod(n, BATCH)
                    outs = [("O", j, 2 * b), ("O", j, 2 * b + 1)] if (j or not first) else []
                    if n == 0:
                        if not first:
                            out_low(-2)
                            probs_low(-1)
                            for o in outs:
                                add_output(number[o], bank_of[o], o[2])
                        rotate(("A", 0, 0))
                        peaks(0)
                        shares(0)
                        continue
                    peaks(n)
                    if not (first and n < 2):
                        out_low(n - 2)
                    probs_low(n - 1)
                    shares(n)
                    if j < PER - 1 or not last:
                        for i in MADE[b]:
                            rotate(("A", j, i))
                    for o in outs:
                        add_output(number[o], bank_of[o], o[2])
                    if n == 1:
                        for i in range(2):
                            plain_low(("V", 0, i))
                        for i in range(4):
                            plain_low(("LVa", 0, i))
                    if n == 9:
                        for i in range(4):
                            plain_low(("LVb", 0, i))
                if last:
                    out_low(STEPS - 2)
                    probs_low(STEPS - 1)
                    out_low(STEPS - 1)
                    for t in range(TT):
                        add_output(TOTAL_UNITS + t, TOTAL_UNITS + t, t)

            groups(dve, body)


def ffn_block(nc, tag, X, XT, banks, WGU, WD):
    with ExitStack() as ctx:
        sb = lambda n, s, d: ctx.enter_context(nc.sbuf_tensor(tag + n, s, d))
        sem = lambda n: ctx.enter_context(nc.semaphore(tag + n))
        W = Pair(ctx, nc, tag + "w", [P, 2, 3, 512])
        H = Pair(ctx, nc, tag + "h", [P, 2, TOK])
        act_gate = sb("act_gate", [P, 2, HALF], F32)
        hidden = sb("hidden", [P, 2, HALF], F32)
        split_hi, split = sem("split_hi"), sem("split")
        gated, silued, product_done = sem("gated"), sem("silued"), sem("product_done")
        h_hi, h_lo, downed, added = sem("h_hi"), sem("h_lo"), sem("downed"), sem("added")
        passed = sem("passed")
        UNITS, PIECES = FT // 2, 3 * FT
        block = ctx.enter_context(nc.Block())

        def pairs(eng, body):
            body(0)
            with eng.Fori(1, UNITS) as g:
                body(g)

        def cells(m, s, parts):
            for i in parts:
                if i < 2:
                    src = WGU[:, :, bass.ds(i * FT * P + m * P, P)]
                    hi, lo = (x[:, s, i, :].rearrange("p (k f) -> p k f", k=KT) for x in (W.hi, W.lo))
                else:
                    src = WD[:, bass.ds(m, 1), :].rearrange("p a d -> p (a d)")
                    hi, lo = W.hi[:, s, i, :], W.lo[:, s, i, :]
                yield src, hi, lo

        def loop(eng, body):
            body(0, False)
            with eng.Fori(1, UNITS - 1) as g:
                body(g, False)
            body(UNITS - 1, True)

        @block.gpsimd
        def _(pool):
            def split_low(number, m, s, parts):
                for i, (src, hi, lo) in enumerate(cells(m, s, parts)):
                    hold(pool, passed, (split_hi, number + i + 1))
                    pool.tensor_tensor(lo, src, hi.bitcast(F32), ALU.subtract).then_inc(split, 1)

            def body(g, last):
                for s in range(2):
                    m = 2 * g + s
                    if not last:
                        split_low(5 + 3 * m, m + 2, s, (0, 1))
                    if not (last and s):
                        split_low(PIECES - 1 if last else 7 + 3 * m, m + 1, 1 - s, (2,))

            for number, m, parts in ((0, 0, (0, 1)), (2, 1, (0, 1)), (4, 0, (2,))):
                split_low(number, m, m, parts)
            loop(pool, body)

        @block.scalar
        def _(act):
            def split_high(m, s, parts):
                for src, hi, _ in cells(m, s, parts):
                    act.activation(hi, src, ACT.Copy).then_inc(split_hi, 1)

            def body(g, last):
                for s in range(2):
                    m = 2 * g + s
                    for h in range(2):
                        wait(act, gated, 2 * m + h + 1)
                        wait(act, product_done, 2 * m + h - 1)
                        act.activation(act_gate[:, h, :], banks[2 * h][:, :], ACT.Silu).then_inc(silued, 1)
                    wait(act, downed, TT * (m - 1))
                    for h in range(2):
                        at = slice(h * HALF, (h + 1) * HALF)
                        wait(act, product_done, 2 * m + h + 1)
                        act.activation(H.hi[:, s, at], hidden[:, h, :], ACT.Copy).then_inc(h_hi, 1)
                    if not last:
                        split_high(m + 2, s, (0, 1))
                    if not (last and s):
                        wait(act, downed, TT * m)
                        split_high(m + 1, 1 - s, (2,))

            for m, parts in ((0, (0, 1)), (1, (0, 1)), (0, (2,))):
                split_high(m, m, parts)
            loop(act, body)

        @block.vector
        def _(dve):
            def body(g):
                for s in range(2):
                    m = 2 * g + s
                    for h in range(2):
                        wait(dve, silued, 2 * m + h + 1)
                        wait(dve, h_lo, 2 * m + h - 1)
                        dve.tensor_tensor(hidden[:, h, :], banks[2 * h + 1][:, :], act_gate[:, h, :], ALU.mult)\
                           .then_inc(product_done, 1)
                    for h in range(2):
                        at = slice(h * HALF, (h + 1) * HALF)
                        wait(dve, h_hi, 2 * m + h + 1)
                        dve.tensor_tensor(H.lo[:, s, at], hidden[:, h, :], H.hi[:, s, at].bitcast(F32),
                                          ALU.subtract).then_inc(h_lo, 1)
                    add(m - 1)
            def add(m):
                if isinstance(m, int) and m < 0:
                    return
                for t in range(TT):
                    wait(dve, downed, TT * m + t + 1)
                    dve.tensor_tensor(X[:, t, :], banks[4 + t % 4][:, :], X[:, t, :], ALU.add)\
                       .then_inc(added, 1)
            pairs(dve, body)
            add(FT - 1)

        @block.tensor
        def _(pe):
            final = lambda m: isinstance(m, int) and m == FT - 1

            def body(g):
                for s in range(2):
                    m = 2 * g + s
                    wait(pe, split, 2 if isinstance(m, int) and m == 0 else 3 * m + 1)
                    for h in range(2):
                        at = slice(h * HALF, (h + 1) * HALF)
                        wait(pe, product_done, 2 * m + h - 1)
                        for i in range(2):
                            for k in range(KT):
                                last = product(pe, banks[2 * h + i][:, :], W[:, s, i, k * P:(k + 1) * P],
                                               XT[:, k, at], k == 0, k == KT - 1)
                        last.then_inc(gated, 1)
                    down(m - 1, 1 - s)
            def down(m, s):
                if isinstance(m, int) and m < 0:
                    return
                wait(pe, split, PIECES if final(m) else 3 * m + 5)
                wait(pe, h_lo, 2 * m + 2)
                for t in range(TT):
                    wait(pe, added, TT * m + t - 3)
                    product(pe, banks[4 + t % 4][:, :], H[:, s, t * P:(t + 1) * P], W[:, s, 2, :], True, True)\
                        .then_inc(downed, 1)
            pairs(pe, body)
            down(FT - 1, 1)


def gptq_block(nc, ident, banks, WGU, WD, q):
    G1, G2 = q["s_gu"].shape[0], q["s_d"].shape[0]
    C = FT * P
    with ExitStack() as ctx:
        sb = lambda n, s, d: ctx.enter_context(nc.sbuf_tensor("q_" + n, s, d))
        sem = lambda n: ctx.enter_context(nc.semaphore("q_" + n))
        packed = sb("packed", [P, 2 * C], U32)
        packed_d = sb("packed_d", [P, 2, D], U32)
        nib = sb("nib", [P, 2, 512], U32)
        diff = sb("diff", [P, 2, 512], F32)
        gi1, gf1 = sb("gi1", [G1, KT * P], I32), sb("gf1", [G1, 2, KT * P], F32)
        gi2 = WGU[0:G2, 0, 0:C].bitcast(I32)
        gf2 = WGU[0:G2, 1, :].rearrange("g (a c) -> g a c", a=2)
        number = sb("number", [16, 1], F32)
        hot1, hot2 = sb("hot1", [G1, KT * P], R32), sb("hot2", [G2, C], R32)
        qz1, qz2 = sb("qz1", [G1, 2, 172], U32), sb("qz2", [G2, D // 8], U32)
        s1 = WD[0:G1, 0:FT // 2, :].rearrange("g t d -> g (t d)")
        z1 = WD[0:G1, FT // 2:FT, :].rearrange("g t d -> g (t d)").bitcast(U32)\
            .rearrange("g (a c) -> g a c", a=2)
        z2 = sb("z2", [G2, D], U32)
        Z1, Z2 = sb("Z1", [G1, 2 * C], R32), sb("Z2", [G2, D], R32)
        s2 = sb("s2", [G2, D], F32)
        S1, S2 = Pair(ctx, nc, "q_S1", [G1, 2 * C]), Pair(ctx, nc, "q_S2", [G2, D])
        landed, chain, ready = sem("landed"), sem("chain"), sem("ready")
        nibbled, differed, spread, dequantised = sem("nibbled"), sem("differed"), sem("spread"), sem("deq")
        chunks = 2 * C // 512
        pieces = [(k, c) for c in range(chunks) for k in range(KT)] + [(None, m) for m in range(FT)]
        block = ctx.enter_context(nc.Block())

        @block.sync
        def _(sp):
            for dst, src in ((packed[0:64, :], q["q_gu"]), (packed[64:P, :], q["q_gu"]),
                             (packed_d[:, :, :], q["q_d"]), (gi1[:, :], q["g_gu"].partition_broadcast(G1)),
                             (gi2, q["g_d"].partition_broadcast(G2)), (number[:, :], q["number"]),
                             (qz1[:, :, :], q["z_gu"]), (qz2[:, :], q["z_d"]), (s1, q["s_gu"]),
                             (s2[:, :], q["s_d"])):
                sp.dma_start(dst, src).then_inc(landed, 16)

        @block.vector
        def _(dve):
            done = [0]

            def link(ins):
                ins.then_inc(chain, 1)
                done[0] += 1
                dve.wait_ge(chain, done[0])

            dve.wait_ge(landed, 160)
            link(dve.memset(z1[:, :, :], 0))
            for gi, gf, hot, n in ((gi1[:, :], gf1, hot1, G1), (gi2, gf2, hot2, G2)):
                link(dve.tensor_scalar(gf[:, 0, :], gi, 0.0, float(n), ALU.is_lt, ALU.mult))
                link(dve.tensor_tensor(gf[:, 1, :], gi, gf[:, 0, :], ALU.add))
                link(dve.tensor_scalar(gf[:, 0, :], gf[:, 1, :], 0.0, float(n - 1), ALU.max, ALU.min))
                dve.tensor_scalar(hot[:, :], gf[:, 0, :], number[0:n, 0:1], None, ALU.is_equal)
            for n in range(8):
                dve.tensor_scalar(z1[:, :, n * P:(n + 1) * P], qz1[:, :, 0:P], 4 * n, 15,
                                  ALU.logical_shift_right, ALU.bitwise_and)
                at = 8 * P + (n // 2) * P + (n % 2) * 64
                dve.tensor_scalar(z1[:, :, at:at + 44], qz1[:, :, P:172], 4 * n, 15,
                                  ALU.logical_shift_right, ALU.bitwise_and)
                ins = dve.tensor_scalar(z2[:, n * 64:(n + 1) * 64], qz2[:, :],
                                        4 * n, 15, ALU.logical_shift_right, ALU.bitwise_and)
            link(ins)
            dve.tensor_scalar(Z1[:, :], z1[:, :, :].rearrange("g a c -> g (a c)"), 1.0, None, ALU.add)
            dve.tensor_scalar(Z2[:, :], z2[:, :], 1.0, None, ALU.add)
            dve.tensor_copy(S1.hi[:, :], s1)
            link(dve.tensor_copy(S2.hi[:, :], s2[:, :]))
            dve.tensor_tensor(S1.lo[:, :], s1, S1.hi[:, :].bitcast(F32), ALU.subtract)
            dve.tensor_tensor(S2.lo[:, :], s2[:, :], S2.hi[:, :].bitcast(F32), ALU.subtract)\
               .then_inc(ready, 1)
            dve.tensor_scalar(packed[64:P, :], packed[64:P, :], 4, None, ALU.logical_shift_right)
            link(dve.tensor_scalar(packed_d[64:P, 1, :], packed_d[64:P, 1, :], 4, None,
                                   ALU.logical_shift_right))
            for i, (k, c) in enumerate(pieces):
                if k is None:
                    src, shift = (packed_d[:, 0, :], 4 * c) if c < 8 else (packed_d[:, 1, :], 8 * (c - 8))
                    dst = WD[:, c, :]
                else:
                    src, shift = packed[:, c * 512:(c + 1) * 512], 8 * k
                    dst = WGU[:, k, c * 512:(c + 1) * 512]
                wait(dve, differed, i - 1)
                dve.tensor_scalar(nib[:, i % 2, :], src, shift, 15, ALU.logical_shift_right, ALU.bitwise_and)\
                   .then_inc(nibbled, 1)
                dve.wait_ge(nibbled, i + 1)
                dve.wait_ge(spread, i + 1)
                wait(dve, dequantised, i - 1)
                dve.tensor_tensor(diff[:, i % 2, :], nib[:, i % 2, :], banks[2 * (i % 2)][:, :], ALU.subtract)\
                   .then_inc(differed, 1)
                dve.wait_ge(differed, i + 1)
                dve.tensor_tensor(dst, diff[:, i % 2, :], banks[2 * (i % 2) + 1][:, :], ALU.mult)\
                   .then_inc(dequantised, 1)

        @block.tensor
        def _(pe):
            pe.wait_ge(ready, 1)
            for i, (k, c) in enumerate(pieces):
                wait(pe, dequantised, i - 1)
                if k is None:
                    hot, at, Z, S = hot2[:, c * P:(c + 1) * P], slice(0, D), Z2, S2
                else:
                    hot, at, Z, S = hot1[:, k * P:(k + 1) * P], slice(c * 512, (c + 1) * 512), Z1, S1
                pe.matmul(banks[2 * (i % 2)][:, :], hot, Z[:, at], start=True, stop=True)
                pe.matmul(banks[2 * (i % 2) + 1][:, :], hot, S.hi[:, at], start=True, stop=False)
                pe.matmul(banks[2 * (i % 2) + 1][:, :], hot, S.lo[:, at], start=False, stop=True)\
                  .then_inc(spread, 1)


NF4 = np.array([-1.0, -0.6961928009986877, -0.5250730514526367, -0.39491748809814453, -0.28444138169288635,
                -0.18477343022823334, -0.09105003625154495, 0.0, 0.07958029955625534, 0.16093020141124725,
                0.24611230194568634, 0.33791524171829224, 0.44070982933044434, 0.5626170039176941,
                0.7229568362236023, 1.0], np.float32)


def nf4_block(nc, ident, banks, WGU, WD, w12, w3):
    bounds = [float(x) for x in (NF4[:-1] + NF4[1:]) * np.float32(0.5)]
    jumps = [float(x) for x in NF4[1:] - NF4[:-1]]
    with ExitStack() as ctx:
        sb = lambda n, s, d: ctx.enter_context(nc.sbuf_tensor("n_" + n, s, d))
        sem = lambda n: ctx.enter_context(nc.semaphore("n_" + n))
        raw = sb("raw", [P, 2, 512], F32)
        unit = sb("unit", [P, 512], F32)
        term = sb("term", [P, 15, 512], F32)
        acc, upper = sb("acc", [P, 512], F32), sb("upper", [P, 512], F32)
        high, low, top = sb("high", [P, 8], F32), sb("low", [P, 8], F32), sb("top", [P, 8], F32)
        safe = sb("safe", [P, 8], F32)
        inv = sb("inv", [P, 8], F32)
        tile12 = sb("tile12", [P, 2, 512], F32)
        tile3 = sb("tile3", [P, 11 * 512], F32)
        landed = [sem("landed0"), sem("landed1")]
        chain, coded, turned, stored = sem("chain"), sem("coded"), sem("turned"), sem("stored")
        zeroed, upper_terms, upper_sum = sem("zeroed"), sem("upper_terms"), sem("upper_sum")
        SHARED = 8
        F12 = 2 * (FT - 1)
        pieces = [(i, m) for m in range(FT - 1) for i in range(2)] + [(2, c) for c in range(11)]
        block = ctx.enter_context(nc.Block())

        @block.sync
        def _(sp):
            for n, (i, m) in enumerate(pieces):
                wait(sp, coded, n - 1)
                src = w12[i, m] if i < 2 else w3[:, m * 512:(m + 1) * 512]
                sp.dma_start(raw[:, n % 2, :], src).then_inc(landed[n % 2], 16)

        @block.vector
        def _(dve):
            done = [0]

            def link(ins):
                ins.then_inc(chain, 1)
                done[0] += 1
                dve.wait_ge(chain, done[0])

            def blocks(x, i):
                if i < 2:
                    return x.rearrange("p (n b r) -> p b n r", n=8, b=8)
                return x.rearrange("p (b n r) -> p b n r", b=8, n=8)

            wide = lambda x: x.unsqueeze(2).unsqueeze(3).to_broadcast([P, 8, 8, 8])
            for n, (i, m) in enumerate(pieces):
                dve.wait_ge(landed[n % 2], 16 * (n // 2 + 1))
                src = raw[:, n % 2, :]
                dve.tensor_reduce(high[:, :], blocks(src, i), AX_XY, ALU.max)
                link(dve.tensor_reduce(low[:, :], blocks(src, i), AX_XY, ALU.min))
                link(dve.scalar_tensor_tensor(out=top[:, :], in0=low[:, :], scalar=-1.0, in1=high[:, :],
                                              op0=ALU.mult, op1=ALU.max))
                link(dve.scalar_tensor_tensor(out=safe[:, :], in0=top[:, :], scalar=0.0, in1=top[:, :],
                                              op0=ALU.is_equal, op1=ALU.add))
                link(dve.reciprocal(inv[:, :], safe[:, :]))
                link(dve.tensor_tensor(blocks(unit[:, :], i), blocks(src, i), wide(inv[:, :]), ALU.mult))
                for k in range(SHARED, 15):
                    ins = dve.tensor_scalar(term[:, k, :], unit[:, :], bounds[k], jumps[k], ALU.is_gt, ALU.mult)
                ins.then_inc(upper_terms, 1)
                for k in range(SHARED):
                    ins = dve.tensor_scalar(term[:, k, :], unit[:, :], bounds[k], jumps[k], ALU.is_gt, ALU.mult)
                link(ins)
                link(dve.tensor_tensor(acc[:, :], term[:, 0, :], term[:, 1, :], ALU.add))
                for k in range(2, SHARED):
                    link(dve.tensor_tensor(acc[:, :], acc[:, :], term[:, k, :], ALU.add))
                dve.wait_ge(upper_sum, (14 - SHARED) * (n + 1))
                link(dve.tensor_tensor(acc[:, :], acc[:, :], upper[:, :], ALU.add))
                if i < 2:
                    wait(dve, turned, n - 1)
                    dst = tile12[:, n % 2, :]
                else:
                    dst = tile3[:, m * 512:(m + 1) * 512]
                link(dve.tensor_scalar(acc[:, :], acc[:, :], -1.0, None, ALU.add))
                dve.tensor_tensor(blocks(dst, i), blocks(acc[:, :], i), wide(top[:, :]), ALU.mult)\
                   .then_inc(coded, 1)
                dve.wait_ge(coded, n + 1)
            dve.memset(WGU[:, :, :].rearrange("p k (i f) -> p k i f", i=2)[:, :, :, INTER:FT * P], 0.0)
            dve.memset(WD[:, FT - 2:FT, :], 0.0).then_inc(zeroed, 1)

        @block.gpsimd
        def _(pool):
            added = 0
            for n in range(len(pieces)):
                pool.wait_ge(upper_terms, n + 1)
                wait(pool, coded, n)
                for k in range(SHARED + 1, 15):
                    if k > SHARED + 1:
                        pool.wait_ge(upper_sum, added)
                    first = term[:, SHARED, :] if k == SHARED + 1 else upper[:, :]
                    pool.tensor_tensor(upper[:, :], first, term[:, k, :], ALU.add).then_inc(upper_sum, 1)
                    added += 1

        @block.tensor
        def _(pe):
            for n in range(F12):
                pe.wait_ge(coded, n + 1)
                wait(pe, stored, n - 1)
                for k in range(KT):
                    last = pe.transpose(banks[n % 2][:, k * P:(k + 1) * P],
                                        tile12[:, n % 2, k * P:(k + 1) * P], ident[:, :])
                last.then_inc(turned, 1)
            pe.wait_ge(coded, len(pieces))
            for m in range(FT - 1):
                n = F12 + m
                rows = min(P, INTER - m * P)
                wait(pe, stored, n - 1)
                for a in range(2):
                    for odd in range(2):
                        at = (2 * a + odd) * INTER + m * P
                        c = (2 * a + odd) * P
                        last = pe.transpose(banks[n % 2][0:rows, c:c + P], tile3[:, at:at + rows],
                                            ident[:, :])
                last.then_inc(turned, 1)

        @block.scalar
        def _(act):
            for n in range(F12):
                i, m = pieces[n]
                rows = min(P, INTER - m * P)
                act.wait_ge(turned, n + 1)
                at = i * FT * P + m * P
                act.activation(WGU[:, :, at:at + rows],
                               banks[n % 2][:, :].rearrange("p (k f) -> p k f", k=KT)[:, :, 0:rows], ACT.Copy)\
                   .then_inc(stored, 1)
            for m in range(FT - 1):
                n = F12 + m
                rows = min(P, INTER - m * P)
                act.wait_ge(turned, n + 1)
                if m == FT - 2:
                    act.wait_ge(zeroed, 1)
                for half in range(2):
                    ins = act.activation(
                        WD[0:rows, m, :].rearrange("f (q o h p) -> f h o q p", q=4, o=2, h=2)[:, half],
                        banks[n % 2][0:rows, half * 256:(half + 1) * 256]
                        .rearrange("f (o p q) -> f o q p", o=2, q=4), ACT.Copy)
                ins.then_inc(stored, 1)


def kernel_program(nc, x, out, w, phases=(0, 1, 2, 3)):
    with ExitStack() as ctx:
        X = ctx.enter_context(nc.sbuf_tensor("X", [P, TT, D], F32))
        ident = ctx.enter_context(nc.sbuf_tensor("ident", [P, P], F32))
        banks = [ctx.enter_context(nc.psum_tensor(f"bank{i}", [P, 512], F32)) for i in range(8)]
        started, stored = ctx.enter_context(nc.semaphore("started")), ctx.enter_context(nc.semaphore("stored"))
        XT = Pair(ctx, nc, "XT", [P, KT, TOK])
        with nc.Block() as block:
            @block.sync
            def _(sp):
                sp.dma_start(X[:, :, :], x.rearrange("(t p) d -> p t d", p=P)).then_inc(started, 16)
                sp.dma_start(ident[:, :], w["ident"]).then_inc(started, 16)
                sp.wait_ge(started, 32)
        if 0 in phases:
            transposed_block(nc, "t0_", X, XT, ident, banks, False)
            with ExitStack() as scope:
                CQ, KC = Pair(scope, nc, "CQ", [P, 2, TOK]), Pair(scope, nc, "KC", [P, TOK])
                CV = Pair(scope, nc, "CV", [P, TT, LAT])
                latent_block(nc, XT, CQ, KC, CV, banks, w["w_down"], w["l0_cos"], w["l0_sin"])
                l0_attention_block(nc, X, CQ, KC, CV, ident, banks, w["l0_n"], w["l0_r"], w["l0_uv"],
                                   w["l0_o"], w["l0_cos"], w["l0_sin"], w["mask"])
        if 1 in phases:
            with ExitStack() as scope:
                WGU = scope.enter_context(nc.sbuf_tensor("WGU0", [P, KT, 2 * FT * P], F32))
                WD = scope.enter_context(nc.sbuf_tensor("WD0", [P, FT, D], F32))
                gptq_block(nc, ident, banks, WGU, WD, w)
                transposed_block(nc, "t1_", X, XT, ident, banks, normalise=0 in phases)
                ffn_block(nc, "f0_", X, XT, banks, WGU, WD)
        if 2 in phases:
            transposed_block(nc, "t2_", X, XT, ident, banks, normalise=1 in phases)
            with ExitStack() as scope:
                LQ = Pair(scope, nc, "LQ", [P, TOK])
                latent_query_block(nc, XT, LQ, banks, w["w_lq"])
                l1_attention_block(nc, X, XT, LQ, ident, banks, w["l1_q"], w["l1_lk"], w["l1_kv"], w["l1_lv"],
                                   w["l1_o"], w["l1_cos"], w["l1_sin"], w["mask"])
        if 3 in phases:
            with ExitStack() as scope:
                WGU = scope.enter_context(nc.sbuf_tensor("WGU1", [P, KT, 2 * FT * P], F32))
                WD = scope.enter_context(nc.sbuf_tensor("WD1", [P, FT, D], F32))
                nf4_block(nc, ident, banks, WGU, WD, w["w12"], w["w3"])
                transposed_block(nc, "t3_", X, XT, ident, banks, normalise=2 in phases)
                ffn_block(nc, "f1_", X, XT, banks, WGU, WD)
        transposed_block(nc, "t4_", X, None, ident, banks, True)
        with nc.Block() as block:
            @block.sync
            def _(sp):
                sp.dma_start(out.rearrange("(t p) d -> p t d", p=P), X[:, :, :]).then_inc(stored, 16)
                sp.wait_ge(stored, 16)


def width_order():
    return np.arange(D).reshape(64, 8).T.reshape(-1)


def laid_out(inputs):
    a = {}
    c = np.ascontiguousarray
    for k, v in inputs.items():
        inputs[k] = np.asarray(v)
    order = width_order()
    a["x"] = inputs["L0_attn_hidden_states"].reshape(TOK, D)[:, order]
    tiles = lambda m, n: c(m[order].reshape(KT, P, n, -1).transpose(2, 1, 0, 3)).reshape(n, P, -1)
    a["w_lq"] = inputs["L1_attn_w_lq"][order]
    a["l1_q"] = tiles(inputs["L1_attn_w_q"], HEADS)
    a["l1_lk"] = c(inputs["L1_attn_w_lk"].reshape(P, GROUPS, PER * HD).transpose(1, 0, 2))
    a["l1_kv"] = c(np.concatenate([tiles(inputs["L1_attn_w_k"], GROUPS), tiles(inputs["L1_attn_w_v"], GROUPS)],
                                  axis=2))
    a["l1_lv"] = tiles(inputs["L1_attn_w_lv"], HEADS // 2)
    a["l1_o"] = c(np.concatenate([inputs["L1_attn_w_o"][:, order].reshape(HEADS, P, D),
                                  inputs["L1_attn_w_lo"][:, order].reshape(HEADS, P, D)], axis=2))
    inv = (1.0 / np.float32(10000.0) ** (np.arange(0, HD, 2, dtype=np.float32) / np.float32(HD)))\
        .astype(np.float32)
    angle = inv[:, None] * np.arange(SEQ, dtype=np.float32)[None, :]
    a["l1_cos"] = np.concatenate([np.cos(angle)] * 2).astype(np.float32)
    a["l1_sin"] = np.concatenate([np.sin(angle), -np.sin(angle)]).astype(np.float32)
    a["w_down"] = np.concatenate([inputs["L0_attn_w_q_down"], inputs["L0_attn_w_kv_down"],
                                  inputs["L0_attn_w_k_rope"]], axis=1)[order]
    nope = inputs["L0_attn_w_q_up_nope"].reshape(QL, HEADS, HD).transpose(1, 2, 0)
    nope = np.concatenate([nope, inputs["L0_attn_w_uk"].reshape(HEADS, HD, LAT)], axis=2)
    a["l0_n"] = c(nope.reshape(HEADS // 2, 2, HD, QL + LAT).transpose(0, 2, 1, 3)).reshape(HEADS // 2, P, -1)
    rope = np.zeros((2 * P, HEADS, ROPE), np.float32)
    rope[0:QL] = inputs["L0_attn_w_q_up_rope"].reshape(QL, HEADS, ROPE)
    a["l0_r"] = c(rope.reshape(2, P, GROUPS, PER, ROPE).transpose(2, 1, 3, 0, 4)).reshape(GROUPS, P, -1)
    a["l0_uv"] = c(inputs["L0_attn_w_uv"].reshape(GROUPS, PER, HD, LAT).transpose(0, 2, 1, 3))\
        .reshape(GROUPS, P, -1)
    a["l0_o"] = c(inputs["L0_attn_w_out"][:, order].reshape(HEADS // 2, 2, P, D).transpose(0, 2, 1, 3))\
        .reshape(HEADS // 2, P, -1)
    freqs = (np.float32(1.0) / np.float32(10000.0) **
             (np.arange(0, ROPE, 2, dtype=np.float32) / np.float32(ROPE))).astype(np.float32)
    waves = np.float32(2.0 * np.pi) / freqs
    ramp = np.clip((waves / np.float32(4096.0) - np.float32(1.0)) / np.float32(31.0), np.float32(0.0),
                   np.float32(1.0)).astype(np.float32)
    inv = (freqs / (np.float32(1.0) - ramp + ramp * np.float32(40.0))).astype(np.float32)
    angle = inv[:, None] * np.arange(SEQ, dtype=np.float32)[None, :]
    one = np.ones((LAT, SEQ), np.float32)
    a["l0_cos"] = np.concatenate([one, np.cos(angle), np.cos(angle)]).astype(np.float32)
    a["l0_sin"] = np.concatenate([one, np.sin(angle), -np.sin(angle)]).astype(np.float32)
    mask = np.zeros((P, SEQ), np.float32)
    mask[:, P:] = np.where(np.arange(P)[None, :] > np.arange(P)[:, None], np.float32(NEG), np.float32(0))
    a["mask"] = mask
    a["ident"] = np.eye(P, dtype=np.float32)
    def folded(m):
        m = m.reshape(*m.shape[:-1], INTER // 8, 8)
        m = np.moveaxis(m, -1, -2)
        head = m[..., 0:P]
        tail = np.zeros((*m.shape[:-1], 64), m.dtype)
        tail[..., 0:INTER // 8 - P] = m[..., P:]
        tail = tail.reshape(*m.shape[:-2], 4, P)
        return np.concatenate([head, tail], axis=-2)

    both = lambda m: np.stack([m[:, 0:INTER], m[:, INTER:]], axis=1)
    a["q_gu"] = folded(both(inputs["L0_ffn_qweight_gu"])).reshape(KT * P // 8, 2 * FT * P)
    a["s_gu"] = folded(both(inputs["L0_ffn_scales_gu"])).reshape(-1, 2 * FT * P)
    a["z_gu"] = inputs["L0_ffn_qzeros_gu"].reshape(-1, 2, INTER // 8)
    rows = inputs["L0_ffn_qweight_down"][:, order]
    q_d = np.zeros((P, 2, D), rows.dtype)
    q_d[:, 0] = rows[0:P]
    q_d[0:INTER // 8 - P, 1] = rows[P:]
    q_d[64:64 + INTER // 8 - P, 1] = rows[P:]
    a["q_d"] = q_d
    a["s_d"], a["z_d"] = inputs["L0_ffn_scales_down"][:, order], inputs["L0_ffn_qzeros_down"]
    a["g_gu"] = c(inputs["L0_ffn_g_idx_gu"].reshape(64, 8).T).reshape(1, D)
    a["g_d"] = folded(inputs["L0_ffn_g_idx_down"]).reshape(1, FT * P)
    a["number"] = np.arange(16, dtype=np.float32).reshape(16, 1)
    w12 = np.zeros((2, (FT - 1) * P, D), np.float32)
    w12[0, 0:INTER], w12[1, 0:INTER] = inputs["L1_ffn_w1"][:, order], inputs["L1_ffn_w2"][:, order]
    a["w12"] = w12.reshape(2, FT - 1, P, D)
    w3 = np.zeros((P, 11 * 512), np.float32)
    w3[:, 0:4 * INTER] = inputs["L1_ffn_w3"].reshape(2, P, 2 * INTER).transpose(1, 0, 2).reshape(P, -1)
    a["w3"] = w3
    return a


def kernel(**inputs):
    import concourse.bacc as bacc
    from concourse.bass_utils import run_bass_kernel_spmd

    nc = bacc.Bacc("TRN2", target_bir_lowering=False, num_devices=1)
    arrays, args = {}, {}
    for name, a in laid_out(dict(inputs)).items():
        arrays[f"in_{name}"] = np.ascontiguousarray(a)
        args[name] = nc.dram_tensor(f"in_{name}", a.shape, mybir.dt.from_np(a.dtype), kind="ExternalInput").ap()
    out = nc.dram_tensor("out_x", (TOK, D), F32, kind="ExternalOutput").ap()
    kernel_program(nc, args["x"], out, args)
    result = run_bass_kernel_spmd(nc, [arrays], core_ids=[0])
    back = np.argsort(width_order())
    return result.results[0]["out_x"][:, back].reshape(BATCH, SEQ, D)
```
